# Optimizing a Trainium2 kernel written in Bass

```python
import numpy as np
import jax
import jax.numpy as jnp

def _softmax(x, axis=-1):
    return jax.nn.softmax(x, axis=axis)

def _gelu(x):
    return jax.nn.gelu(x, approximate=True)

def _silu(x):
    return jax.nn.silu(x)

def _sigmoid(x):
    return jax.nn.sigmoid(x)

def _layernorm(x, axis=-1, eps=1e-05):
    m = jnp.mean(x, axis=axis, keepdims=True)
    v = jnp.var(x, axis=axis, keepdims=True)
    return (x - m) / jnp.sqrt(v + eps)

def _scatter_add(tgt, idx, src, axis=0):
    return tgt.at[idx].add(src)

def _segment_sum(src, seg, n):
    return jax.ops.segment_sum(src, seg, n)
kernel_name = 'mk_macaron_d1_jaxref_r8_7cb82f'

def setup_inputs(seed: int=0):
    np.random.seed(seed)
    _w = jnp.asarray

    def _L0_attn_setup():
        import jax, jax.numpy as jnp
        import numpy as np
        DIM = 128
        HEADS = 16
        HIDDEN = 512
        EPS_ATTN = 1e-06
        EPS_LN = 1e-05

        def layer_norm(x, g, b):
            mu = jnp.mean(x, axis=-1, keepdims=True)
            var = jnp.var(x, axis=-1, keepdims=True)
            return (x - mu) * jax.lax.rsqrt(var + EPS_LN) * g + b
        key = jax.random.key(seed)
        ks = jax.random.split(key, 8)
        s = 0.02
        return {'x': jax.random.normal(ks[0], (4, 512, DIM), jnp.float32), 'norm1_g': jnp.ones((DIM,), jnp.float32), 'norm1_b': jnp.zeros((DIM,), jnp.float32), 'qkv_w': jax.random.normal(ks[1], (3 * DIM, DIM), jnp.float32) * s, 'proj_w': jax.random.normal(ks[2], (DIM, DIM), jnp.float32) * s, 'proj_b': jnp.zeros((DIM,), jnp.float32), 'norm2_g': jnp.ones((DIM,), jnp.float32), 'norm2_b': jnp.zeros((DIM,), jnp.float32), 'fc1_w': jax.random.normal(ks[3], (HIDDEN, DIM), jnp.float32) * s, 'fc1_b': jnp.zeros((HIDDEN,), jnp.float32), 'fc2_w': jax.random.normal(ks[4], (DIM, HIDDEN), jnp.float32) * s, 'fc2_b': jnp.zeros((DIM,), jnp.float32)}
    _L0_attn_in = _L0_attn_setup()

    def _L0_ffn_setup():
        import jax, jax.numpy as jnp
        import numpy as np
        DIM = 128
        DEPTH = 6
        HEADS = 16
        DIM_HEAD = 64
        WINDOW = 32
        INNER = HEADS * DIM_HEAD
        DIM_INNER = int(DIM * 4 * 2 / 3)
        QK_SCALE = 8.0

        def shift_tokens(t):
            a, s = jnp.split(t, 2, -1)
            s = jnp.pad(s, ((0, 0), (1, 0), (0, 0)))[:, :-1]
            return jnp.concatenate([a, s], -1)

        def l2norm(t):
            return t / jnp.maximum(jnp.linalg.norm(t, axis=-1, keepdims=True), 1e-12)

        def rotate_half(x):
            x1, x2 = jnp.split(x, 2, -1)
            return jnp.concatenate([-x2, x1], -1)

        def rotary_tables(n):
            half = jnp.arange(0, DIM_HEAD, 2, dtype=jnp.float32)
            inv_freq = 1.0 / 10000.0 ** (half / DIM_HEAD)
            t = jnp.arange(n, dtype=jnp.float32)
            freqs = t[:, None] * inv_freq[None, :]
            freqs = jnp.concatenate([freqs, freqs], -1)
            base_scale = (half + 0.4 * DIM_HEAD) / (1.4 * DIM_HEAD)
            power = (t - n // 2) / (WINDOW // 2)
            scale = base_scale[None, :] ** power[:, None]
            scale = jnp.concatenate([scale, scale], -1)
            return (freqs, scale)

        def local_attention(q, k, v):
            b, h, n, d = q.shape
            w = WINDOW
            nw = n // w
            bq = q.reshape(b, h, nw, w, d)
            bk = k.reshape(b, h, nw, w, d)
            bv = v.reshape(b, h, nw, w, d)

            def look(t):
                p = jnp.pad(t, ((0, 0), (0, 0), (1, 0), (0, 0), (0, 0)))
                return jnp.concatenate([p[:, :, :nw], p[:, :, 1:]], axis=3)
            bk2, bv2 = (look(bk), look(bv))
            seq = jnp.arange(n).reshape(nw, w)
            seq_p = jnp.pad(seq, ((1, 0), (0, 0)), constant_values=-1)
            jt = jnp.concatenate([seq_p[:nw], seq_p[1:]], axis=1)
            it = seq[:, :, None]
            jb = jt[:, None, :]
            mask = (it < jb) | (it > jb + w) | (jb == -1)
            sim = jnp.einsum('bhwie,bhwje->bhwij', bq, bk2) * QK_SCALE
            sim = jnp.where(mask, -jnp.finfo(sim.dtype).max, sim)
            attn = jax.nn.softmax(sim, -1)
            out = jnp.einsum('bhwij,bhwje->bhwie', attn, bv2)
            return out.reshape(b, h, n, d)

        def attn_layer(x, Wqkv, qs, ksc, Wo):
            b, n, _ = x.shape
            qkv = x @ Wqkv
            q, k, v = jnp.split(qkv, 3, -1)
            sh = lambda t: t.reshape(b, n, HEADS, DIM_HEAD).transpose(0, 2, 1, 3)
            q, k, v = (sh(q), sh(k), sh(v))
            q = l2norm(q) * qs
            k = l2norm(k) * ksc
            freqs, scale = rotary_tables(n)
            cos, sin = (jnp.cos(freqs), jnp.sin(freqs))
            q = q * cos * scale + rotate_half(q) * sin * scale
            inv = 1.0 / scale
            k = k * cos * inv + rotate_half(k) * sin * inv
            out = local_attention(q, k, v)
            out = out.transpose(0, 2, 1, 3).reshape(b, n, INNER)
            return out @ Wo

        def ffn_layer(x, g, bln, W1, b1, W2, b2):
            mu = x.mean(-1, keepdims=True)
            var = ((x - mu) ** 2).mean(-1, keepdims=True)
            xn = (x - mu) / jnp.sqrt(var + 1e-05) * g + bln
            hg = xn @ W1 + b1
            a, gate = jnp.split(hg, 2, -1)
            return a * jax.nn.gelu(gate, approximate=False) @ W2 + b2
        key = jax.random.key(seed)
        ks = jax.random.split(key, 8)
        B, N = (2, 256)
        init = lambda k, shape: jax.random.normal(k, shape, jnp.float32) * 0.02
        return {'x': jax.random.normal(ks[0], (B, N, DIM), jnp.float32), 'Wqkv': init(ks[1], (DEPTH, DIM, 3 * INNER)), 'q_scale': jnp.ones((DEPTH, DIM_HEAD), jnp.float32), 'k_scale': jnp.ones((DEPTH, DIM_HEAD), jnp.float32), 'Wo': init(ks[2], (DEPTH, INNER, DIM)), 'ln_g': jnp.ones((DEPTH, DIM), jnp.float32), 'ln_b': jnp.zeros((DEPTH, DIM), jnp.float32), 'W1': init(ks[3], (DEPTH, DIM, 2 * DIM_INNER)), 'b1': jnp.zeros((DEPTH, 2 * DIM_INNER), jnp.float32), 'W2': init(ks[4], (DEPTH, DIM_INNER, DIM)), 'b2': jnp.zeros((DEPTH, DIM), jnp.float32)}
    _L0_ffn_in = _L0_ffn_setup()
    _d = {'L0_attn_x': _L0_attn_in['x'], 'L0_attn_norm1_g': _L0_attn_in['norm1_g'], 'L0_attn_norm1_b': _L0_attn_in['norm1_b'], 'L0_attn_qkv_w': _L0_attn_in['qkv_w'], 'L0_attn_proj_w': _L0_attn_in['proj_w'], 'L0_attn_proj_b': _L0_attn_in['proj_b'], 'L0_attn_norm2_g': _L0_attn_in['norm2_g'], 'L0_attn_norm2_b': _L0_attn_in['norm2_b'], 'L0_attn_fc1_w': _L0_attn_in['fc1_w'], 'L0_attn_fc1_b': _L0_attn_in['fc1_b'], 'L0_attn_fc2_w': _L0_attn_in['fc2_w'], 'L0_attn_fc2_b': _L0_attn_in['fc2_b'], 'L0_ffn_Wqkv': _L0_ffn_in['Wqkv'], 'L0_ffn_q_scale': _L0_ffn_in['q_scale'], 'L0_ffn_k_scale': _L0_ffn_in['k_scale'], 'L0_ffn_Wo': _L0_ffn_in['Wo'], 'L0_ffn_ln_g': _L0_ffn_in['ln_g'], 'L0_ffn_ln_b': _L0_ffn_in['ln_b'], 'L0_ffn_W1': _L0_ffn_in['W1'], 'L0_ffn_b1': _L0_ffn_in['b1'], 'L0_ffn_W2': _L0_ffn_in['W2'], 'L0_ffn_b2': _L0_ffn_in['b2']}
    _x0 = _d['L0_attn_x']
    _d['L0_attn_x'] = jax.random.normal(jax.random.fold_in(jax.random.key(seed), 1), (1, 2048, 128), dtype=_x0.dtype)
    del _x0
    return _d

def reference(L0_attn_x, L0_attn_norm1_g, L0_attn_norm1_b, L0_attn_qkv_w, L0_attn_proj_w, L0_attn_proj_b, L0_attn_norm2_g, L0_attn_norm2_b, L0_attn_fc1_w, L0_attn_fc1_b, L0_attn_fc2_w, L0_attn_fc2_b, L0_ffn_Wqkv, L0_ffn_q_scale, L0_ffn_k_scale, L0_ffn_Wo, L0_ffn_ln_g, L0_ffn_ln_b, L0_ffn_W1, L0_ffn_b1, L0_ffn_W2, L0_ffn_b2):

    def _L0_attn_ref(x, norm1_g, norm1_b, qkv_w, proj_w, proj_b, norm2_g, norm2_b, fc1_w, fc1_b, fc2_w, fc2_b):
        import jax, jax.numpy as jnp
        import numpy as np
        DIM = 128
        HEADS = 16
        HIDDEN = 512
        EPS_ATTN = 1e-06
        EPS_LN = 1e-05

        def layer_norm(x, g, b):
            mu = jnp.mean(x, axis=-1, keepdims=True)
            var = jnp.var(x, axis=-1, keepdims=True)
            return (x - mu) * jax.lax.rsqrt(var + EPS_LN) * g + b
        B, N, C = x.shape
        H = HEADS
        d = C // H
        h = layer_norm(x, norm1_g, norm1_b)
        qkv = jnp.einsum('bnc,oc->bno', h, qkv_w)
        qkv = qkv.reshape(B, N, 3, H, d)
        q = jnp.transpose(qkv[:, :, 0], (0, 2, 1, 3))
        k = jnp.transpose(qkv[:, :, 1], (0, 2, 1, 3))
        v = jnp.transpose(qkv[:, :, 2], (0, 2, 1, 3))
        q = jax.nn.elu(q) + 1.0
        k = jax.nn.elu(k) + 1.0
        kv = jnp.einsum('bhnd,bhne->bhde', k, v)
        ksum = jnp.sum(k, axis=2)
        z = 1.0 / (jnp.einsum('bhnd,bhd->bhn', q, ksum) + EPS_ATTN)
        attn_out = jnp.einsum('bhnd,bhde->bhne', q, kv) * z[..., None]
        attn_out = jnp.transpose(attn_out, (0, 2, 1, 3)).reshape(B, N, C)
        attn_out = jnp.einsum('bnc,oc->bno', attn_out, proj_w) + proj_b
        x = x + attn_out
        h = layer_norm(x, norm2_g, norm2_b)
        h = jax.nn.gelu(jnp.einsum('bnc,hc->bnh', h, fc1_w) + fc1_b, approximate=False)
        h = jnp.einsum('bnh,ch->bnc', h, fc2_w) + fc2_b
        return x + h

    def _L0_ffn_ref(x, Wqkv, q_scale, k_scale, Wo, ln_g, ln_b, W1, b1, W2, b2):
        import jax, jax.numpy as jnp
        import numpy as np
        DIM = 128
        DEPTH = 6
        HEADS = 16
        DIM_HEAD = 64
        WINDOW = 32
        INNER = HEADS * DIM_HEAD
        DIM_INNER = int(DIM * 4 * 2 / 3)
        QK_SCALE = 8.0

        def shift_tokens(t):
            a, s = jnp.split(t, 2, -1)
            s = jnp.pad(s, ((0, 0), (1, 0), (0, 0)))[:, :-1]
            return jnp.concatenate([a, s], -1)

        def l2norm(t):
            return t / jnp.maximum(jnp.linalg.norm(t, axis=-1, keepdims=True), 1e-12)

        def rotate_half(x):
            x1, x2 = jnp.split(x, 2, -1)
            return jnp.concatenate([-x2, x1], -1)

        def rotary_tables(n):
            half = jnp.arange(0, DIM_HEAD, 2, dtype=jnp.float32)
            inv_freq = 1.0 / 10000.0 ** (half / DIM_HEAD)
            t = jnp.arange(n, dtype=jnp.float32)
            freqs = t[:, None] * inv_freq[None, :]
            freqs = jnp.concatenate([freqs, freqs], -1)
            base_scale = (half + 0.4 * DIM_HEAD) / (1.4 * DIM_HEAD)
            power = (t - n // 2) / (WINDOW // 2)
            scale = base_scale[None, :] ** power[:, None]
            scale = jnp.concatenate([scale, scale], -1)
            return (freqs, scale)

        def local_attention(q, k, v):
            b, h, n, d = q.shape
            w = WINDOW
            nw = n // w
            bq = q.reshape(b, h, nw, w, d)
            bk = k.reshape(b, h, nw, w, d)
            bv = v.reshape(b, h, nw, w, d)

            def look(t):
                p = jnp.pad(t, ((0, 0), (0, 0), (1, 0), (0, 0), (0, 0)))
                return jnp.concatenate([p[:, :, :nw], p[:, :, 1:]], axis=3)
            bk2, bv2 = (look(bk), look(bv))
            seq = jnp.arange(n).reshape(nw, w)
            seq_p = jnp.pad(seq, ((1, 0), (0, 0)), constant_values=-1)
            jt = jnp.concatenate([seq_p[:nw], seq_p[1:]], axis=1)
            it = seq[:, :, None]
            jb = jt[:, None, :]
            mask = (it < jb) | (it > jb + w) | (jb == -1)
            sim = jnp.einsum('bhwie,bhwje->bhwij', bq, bk2) * QK_SCALE
            sim = jnp.where(mask, -jnp.finfo(sim.dtype).max, sim)
            attn = jax.nn.softmax(sim, -1)
            out = jnp.einsum('bhwij,bhwje->bhwie', attn, bv2)
            return out.reshape(b, h, n, d)

        def attn_layer(x, Wqkv, qs, ksc, Wo):
            b, n, _ = x.shape
            qkv = x @ Wqkv
            q, k, v = jnp.split(qkv, 3, -1)
            sh = lambda t: t.reshape(b, n, HEADS, DIM_HEAD).transpose(0, 2, 1, 3)
            q, k, v = (sh(q), sh(k), sh(v))
            q = l2norm(q) * qs
            k = l2norm(k) * ksc
            freqs, scale = rotary_tables(n)
            cos, sin = (jnp.cos(freqs), jnp.sin(freqs))
            q = q * cos * scale + rotate_half(q) * sin * scale
            inv = 1.0 / scale
            k = k * cos * inv + rotate_half(k) * sin * inv
            out = local_attention(q, k, v)
            out = out.transpose(0, 2, 1, 3).reshape(b, n, INNER)
            return out @ Wo

        def ffn_layer(x, g, bln, W1, b1, W2, b2):
            mu = x.mean(-1, keepdims=True)
            var = ((x - mu) ** 2).mean(-1, keepdims=True)
            xn = (x - mu) / jnp.sqrt(var + 1e-05) * g + bln
            hg = xn @ W1 + b1
            a, gate = jnp.split(hg, 2, -1)
            return a * jax.nn.gelu(gate, approximate=False) @ W2 + b2
        for i in range(DEPTH):
            x = attn_layer(shift_tokens(x), Wqkv[i], q_scale[i], k_scale[i], Wo[i]) + x
            x = ffn_layer(shift_tokens(x), ln_g[i], ln_b[i], W1[i], b1[i], W2[i], b2[i]) + x
        return x
    x = L0_attn_x
    x = x + 0.5 * _L0_ffn_ref(_layernorm(x, axis=-1), L0_ffn_Wqkv, L0_ffn_q_scale, L0_ffn_k_scale, L0_ffn_Wo, L0_ffn_ln_g, L0_ffn_ln_b, L0_ffn_W1, L0_ffn_b1, L0_ffn_W2, L0_ffn_b2)
    x = x + _L0_attn_ref(_layernorm(x, axis=-1), L0_attn_norm1_g, L0_attn_norm1_b, L0_attn_qkv_w, L0_attn_proj_w, L0_attn_proj_b, L0_attn_norm2_g, L0_attn_norm2_b, L0_attn_fc1_w, L0_attn_fc1_b, L0_attn_fc2_w, L0_attn_fc2_b)
    x = x + 0.5 * _L0_ffn_ref(_layernorm(x, axis=-1), L0_ffn_Wqkv, L0_ffn_q_scale, L0_ffn_k_scale, L0_ffn_Wo, L0_ffn_ln_g, L0_ffn_ln_b, L0_ffn_W1, L0_ffn_b1, L0_ffn_W2, L0_ffn_b2)
    return x

_drawn_inputs = setup_inputs


def setup_inputs(seed=0):
    import zlib

    import numpy as np

    out = dict(_drawn_inputs(seed))
    spreads = {'L0_attn_norm1_g': (1.0, 0.6),
     'L0_attn_norm1_b': (0.0, 0.8),
     'L0_attn_proj_b': (0.0, 0.463),
     'L0_attn_norm2_g': (1.0, 0.6),
     'L0_attn_norm2_b': (0.0, 2.0),
     'L0_attn_fc1_b': (0.0, 0.8),
     'L0_attn_fc2_b': (0.0, 0.488),
     'L0_ffn_q_scale': (1.0, 0.6),
     'L0_ffn_k_scale': (1.0, 0.6),
     'L0_ffn_ln_g': (1.0, 0.6),
     'L0_ffn_ln_b': (0.0, 0.8),
     'L0_ffn_b1': (0.0, 0.8),
     'L0_ffn_b2': (0.0, 0.1)}
    factors = {'L0_attn_qkv_w': 8.0,
     'L0_attn_proj_w': 8.0,
     'L0_ffn_W1': 3.649,
     'L0_ffn_W2': 3.584,
     'L0_attn_fc1_w': 2.785}
    for name, (base, spread) in spreads.items():
        noise = np.random.default_rng([zlib.crc32(name.encode()), seed]).standard_normal(out[name].shape)
        drawn = base * np.exp(spread * noise) if base else spread * noise
        out[name] = jnp.asarray(drawn.astype(out[name].dtype))
    for name, factor in factors.items():
        out[name] = (out[name] * factor).astype(out[name].dtype)
    return out
```

```python
from contextlib import ExitStack

import numpy as np

import concourse.bass as bass
from concourse import mybir

F32 = mybir.dt.float32
BF16 = mybir.dt.bfloat16
I32 = mybir.dt.int32
ALU = mybir.AluOpType
ACT = mybir.ActivationFunctionType
AX = mybir.AxisListType

P = 128
NTOK = 2048
CH = 16
GT = 512
NG = NTOK // GT
DEPTH = 6
HEADS = 16
DH = 64
NP_ = HEADS // 2
WIN = 32
NW = P // WIN
DI = 341
FT = [(0, 114), (114, 114), (228, 113)]
MH = 8
EPS = 1e-5
QK_SCALE = 8.0
MASKED = -1.0e30
RSQRT_MAGIC = float(0x5F3759DF)

RAW, TQ, TK, SB, OB = 0, 2, 3, 4, 6
CEN, VAR, RB, HB, YB = 0, 1, 2, 3, 7

S_G, S_B, S_B2, S_B1A, S_B1G, NSMALL = 0, 1, 2, 3, 6, 9
M_G1, M_B1, M_PB, M_G2, M_B2, M_FC2B, M_FC1B, NMSMALL = 0, 1, 2, 3, 4, 5, 6, 10


def shape_constants():
    half = np.arange(0, DH, 2, dtype=np.float32)
    inv_freq = (1.0 / np.float32(10000.0) ** (half / np.float32(DH))).astype(np.float32)
    tok = np.arange(NTOK, dtype=np.float32)
    freqs = (tok[:, None] * inv_freq[None, :]).astype(np.float32).astype(np.float64)
    base = ((half + np.float32(0.4 * DH)) / np.float32(1.4 * DH)).astype(np.float32).astype(np.float64)
    power = (np.arange(NTOK) % P) / (WIN // 2)
    scale = base[None, :] ** power[:, None]
    cos, sin = np.cos(freqs), np.sin(freqs)
    rot = np.concatenate(
        [np.concatenate([cos, cos, -sin, sin], 1) * np.tile(s, 4) for s in (scale, 1.0 / scale)], 1)
    rot = rot.astype(np.float32).reshape(CH, P, 4 * DH).transpose(1, 0, 2)
    to_next = np.tile(base ** (P / (WIN // 2)), 4).astype(np.float32).reshape(P, 1)
    q, k = np.arange(P)[:, None] % WIN, np.arange(2 * WIN)[None, :]
    seen = (k - WIN <= q) & (q <= k)
    first = seen & ((k >= WIN) | (np.arange(P)[:, None] >= WIN))
    masks = np.stack([np.where(m, 0.0, MASKED) for m in (seen, first)], 1).astype(np.float32)
    blocks = (np.arange(P)[:, None] // MH == np.arange(P)[None, :] // MH).astype(np.float32)
    eye = np.eye(P, dtype=np.float32)
    return {
        "c_rot": np.ascontiguousarray(rot.reshape(P, CH * 4 * DH)),
        "c_next": to_next,
        "c_masks": np.ascontiguousarray(masks.reshape(P, 4 * WIN)),
        "c_blocks": blocks,
        "c_eye": eye,
        "c_center": (eye - np.float32(1.0 / P)).astype(np.float32),
    }


def build(nc, a, out):
    ctx = ExitStack()
    with ctx:
        def sb(name, shape, dt=F32):
            return ctx.enter_context(nc.sbuf_tensor(name, shape, dt))

        def sem(name):
            return ctx.enter_context(nc.semaphore(name))

        XR = sb("XR", [P, NTOK])
        XA = sb("XA", [P, NTOK + 1])
        XB = sb("XB", [P, NTOK + 1])
        ROT = sb("ROT", [P, CH, 4 * DH])
        NEXT = sb("NEXT", [P, 1])
        MASKF = sb("MASKF", [P, 2, 2 * WIN])
        MASK = sb("MASK", [P, 2, 2 * WIN], BF16)
        EYE = sb("EYE", [P, P])
        EYEB = sb("EYEB", [P, P], BF16)
        CENTER = sb("CENTER", [P, P])
        BLOCKS = sb("BLOCKS", [P, P])
        ONES = sb("ONES", [P, P])
        MEAN = sb("MEAN", [P, 1])
        WQKV = sb("WQKV", [P, 3 * HEADS * DH])
        WO = sb("WO", [P, NP_, P])
        QKS = sb("QKS", [P, 4 * DH])
        W1 = sb("W1", [P, 2 * DI])
        W2 = sb("W2", [P, 3, P])
        SMALL = sb("SMALL", [P, NSMALL])
        XS = sb("XS", [P, 2, P])
        RAWQK = sb("RAWQK", [P, 2, HEADS, DH])
        SQ = sb("SQ", [P, 2, HEADS, DH])
        SS = sb("SS", [P, 2 * HEADS])
        NX = sb("NX", [P, 2 * HEADS])
        NU = sb("NU", [P, 2 * HEADS])
        RN = sb("RN", [P, 2, HEADS])
        TAB = sb("TAB", [P, 4 * DH])
        QN = sb("QN", [P, 2, HEADS, DH])
        U = sb("U", [P, 2, HEADS, DH])
        V = sb("V", [P, 2, HEADS, DH])
        QT = sb("QT", [P, 2, NP_, P])
        KT = sb("KT", [P, 2, NP_, WIN + P])
        MX = sb("MX", [P, HEADS])
        SM = sb("SM", [P, 2, HEADS, 2 * WIN])
        SUM = sb("SUM", [P, 2, HEADS])
        PR = sb("PR", [P, HEADS, 2 * WIN])
        PT = sb("PT", [P, NP_, P])
        VS = sb("VS", [P, 2, HEADS * DH])
        V2 = sb("V2", [P, 2, NW, NP_ * DH])
        OT = sb("OT", [P, NP_, P])
        XF = sb("XF", [P, GT])
        D2 = QT[:, 0, 0:4, :].rearrange("p a b -> p (a b)")
        DG = QT[:, 0, 4:8, :].rearrange("p a b -> p (a b)")
        DIAG = QT[:, 1, 0:4, :].rearrange("p a b -> p (a b)")
        V4 = sb("V4", [P, 4])
        NX4 = sb("NX4", [P, 4])
        NU4 = sb("NU4", [P, 4])
        R4 = sb("R4", [P, 4])
        XN = sb("XN", [P, 2, GT])
        gb_ = U[:, :, :, :].rearrange("p a b c -> p (a b c)")
        ht_ = V[:, :, :, :].rearrange("p a b c -> p (a b c)")
        GB = gb_.rearrange("p (i t) -> p i t", t=GT)
        HT = ht_.rearrange("p (i t) -> p i t", t=GT)
        XIO = QN[:, :, :, :].rearrange("p a b c -> p (a b c)").rearrange("p (c d) -> p c d", d=P)
        WQ_M = QKS[:, 0:P]
        WQM = sb("WQM", [P, P])
        WKVM = sb("WKVM", [P, 2 * P])
        PROJ = sb("PROJ", [P, P])
        FC1 = sb("FC1", [P, 4 * P])
        FC2 = sb("FC2", [P, 4, P])
        MSMALL = sb("MSMALL", [P, NMSMALL])
        QB = RAWQK[:, :, :, :].rearrange("p a b c -> p (a b c)")
        EL = SQ[:, 0, :, :].rearrange("p a b -> p (a b)")[:, 0:GT]
        K4 = SM[:, 0, :, :].rearrange("p a b -> p (a b)")[:, 0:GT].rearrange("p (j d) -> p j d", d=P)
        VX = sb("VX", [P, 4, P + 1])
        KVM = PR[:, 0:2, :].rearrange("p a b -> p (a b)")
        KSM = PR[:, 2:4, :].rearrange("p a b -> p (a b)")
        KS1 = sb("KS1", [P, 1])

        PS = ctx.enter_context(nc.psum_tensor("PS", [P, 8, 512], F32))

        consts = sem("consts"); init = sem("init"); cast = sem("cast")
        attn_w = sem("attn_w"); ffn_w = sem("ffn_w"); mid_w = sem("mid_w")
        xs_ready = sem("xs_ready"); tab_ready = sem("tab_ready")
        raw_q = sem("raw_q"); raw_k = sem("raw_k"); raw_v = sem("raw_v")
        sq_q = sem("sq_q"); sq_k = sem("sq_k"); v_evac = sem("v_evac")
        qn_ready = sem("qn_ready"); u_ready = sem("u_ready"); vv_ready = sem("vv_ready")
        t0_ready = sem("t0_ready"); t1_ready = sem("t1_ready")
        tev0 = sem("tev0"); tev1 = sem("tev1"); halo_ready = sem("halo_ready")
        s_ready = sem("s_ready"); sm_ready = sem("sm_ready"); e_ready = sem("e_ready")
        rs_ready = sem("rs_ready"); p_ready = sem("p_ready")
        pt_ready = sem("pt_ready"); ptev = sem("ptev")
        v2_even = sem("v2_even"); v2_odd = sem("v2_odd")
        o_ready = sem("o_ready"); otev = sem("otev"); wo_ready = sem("wo_ready"); xb_ready = sem("xb_ready")
        xa_ready = sem("xa_ready")
        xf_ready = sem("xf_ready"); cen_ready = sem("cen_ready"); d2_ready = sem("d2_ready")
        dg_ready = sem("dg_ready"); var_ready = sem("var_ready"); r4_ready = sem("r4_ready")
        diag_ready = sem("diag_ready"); rb_ready = sem("rb_ready"); ln_done = sem("ln_done")
        h_ready = sem("h_ready"); gelu_ready = sem("gelu_ready"); ht_ready = sem("ht_ready"); y_ready = sem("y_ready")
        x_in = sem("x_in"); xt_ready = sem("xt_ready"); xr_ready = sem("xr_ready")
        mq_ready = sem("mq_ready"); mkv_ready = sem("mkv_ready"); el_q = sem("el_q"); el_k = sem("el_k")
        ex_q = sem("ex_q"); ex_k = sem("ex_k"); mq_done = sem("mq_done"); k4_ready = sem("k4_ready")
        vx_ready = sem("vx_ready"); kv_ready = sem("kv_ready"); kvm_ready = sem("kvm_ready")
        num_ready = sem("num_ready"); ao_ready = sem("ao_ready"); proj_ready = sem("proj_ready")
        x1_ready = sem("x1_ready"); mh_ready = sem("mh_ready"); mg_ready = sem("mg_ready")
        my_ready = sem("my_ready"); xr_mid = sem("xr_mid"); xr_half = sem("xr_half")
        o_t = sem("o_t"); o_c = sem("o_c"); stored = sem("stored")

        def lncount(inv):
            return 4 if inv == 0 else 4 + 4 * DEPTH + 12 + 4

        A_DMAS, F_DMAS, V2_DMAS = 3, 4, 16
        V2_INC = 16 * V2_DMAS

        def split(ap):
            return ap.rearrange("p (r j) d -> p r j d", r=2)

        def paired(ap):
            return ap.rearrange("p (j r) d -> p r j d", r=2)

        def per_dim(ap, n):
            return ap.unsqueeze(1).unsqueeze(1).broadcast_to([P, 2, NP_, n])

        def rep(ap, shape, axis):
            return ap.unsqueeze(axis).broadcast_to(shape)

        block = ctx.enter_context(nc.Block())

        def layers(eng, attn_step, attn_start, ffn, layer_end=None):
            def stack(inv):
                with eng.Fori(0, DEPTH) as lay:
                    first = eng.snap(lay * CH + inv * DEPTH * CH)

                    def counter(start):
                        kept = {}

                        def count(k):
                            if k not in kept:
                                kept[k] = eng.snap(start + k)
                            return kept[k]
                        return count

                    def v2count(pairs):
                        return eng.snap(lay * (CH // 2 * V2_INC) + (inv * DEPTH * CH // 2 + pairs) * V2_INC)

                    attn_start(inv, lay)
                    for i in (0, 1):
                        attn_step(i, i, counter(first + i), lambda k: v2count(k), True, i >= 1, False, i == 1)
                    with eng.Fori(0, CH // 2 - 1) as j:
                        at = eng.snap(first + j * 2)
                        c = counter(at + 2)
                        v2j = eng.snap(lay * (CH // 2 * V2_INC) + j * V2_INC + (inv * DEPTH * CH // 2) * V2_INC)
                        for p in (0, 1):
                            attn_step(p, eng.snap(j * 2 + (2 + p)), lambda k, p=p: c(k + p),
                                      lambda k: eng.snap(v2j + (k + 1) * V2_INC), True, True, True, False)
                    c = counter(first + CH)
                    v = lambda k: v2count(k + CH // 2)
                    attn_step(0, CH, c, v, False, True, True, False)
                    attn_step(1, CH + 1, lambda k: c(k + 1), v, False, False, True, False)
                    ffn(inv, lay)
            return stack

        @block.tensor
        def _(pe):
            pe.wait_ge(consts, 16 * 6)
            pe.wait_ge(init, 5)
            pe.wait_ge(cast, 1)
            pe.wait_ge(x_in, 16)
            for c in range(CH):
                mm = pe.transpose(PS[:, c // 4, (c % 4) * P:(c % 4 + 1) * P], XIO[:, c, :], EYE[:, :])
                if c % 4 == 3:
                    mm.then_inc(xt_ready, 1)

            def ln_center(v, rhs, ready, value, prev=True):
                pe.wait_ge(ready, value)
                if prev:
                    pe.wait_ge(dg_ready, v)
                pe.matmul(PS[:, CEN, :], CENTER[:, :], rhs, start=True, stop=True).then_inc(cen_ready, 1)

            def ln_var(v, prev=True):
                pe.wait_ge(d2_ready, v + 1)
                if prev:
                    pe.wait_ge(r4_ready, v)
                for j in range(4):
                    mm = pe.matmul(PS[:, VAR, j:j + 1], D2[:, j * P:(j + 1) * P], MEAN[:, :], start=True, stop=True)
                mm.then_inc(var_ready, 1)

            def ln_spread(v, prev=True):
                pe.wait_ge(diag_ready, v + 1)
                if prev:
                    pe.wait_ge(ln_done, v)
                pe.matmul(PS[:, RB, :], ONES[:, :], DIAG, start=True, stop=True).then_inc(rb_ready, 1)

            def ln(v, rhs, ready, value):
                ln_center(v, rhs, ready, value)
                ln_var(v)
                ln_spread(v)

            def attn_start(inv, lay):
                pe.wait_ge(attn_w, pe.snap(lay * (16 * A_DMAS) + (inv * DEPTH + 1) * 16 * A_DMAS))

            def project(part, p, done):
                for b in range(2):
                    at = (2 * part + b) * 512
                    mm = pe.matmul(PS[:, RAW + b, :], XS[:, p, :], WQKV[:, at:at + 512], start=True, stop=True)
                mm.then_inc(done, 1)

            def turn(g, p, done):
                for qk in range(2):
                    for j in range(4):
                        pair = 4 * g + j
                        o = PS[:, TQ + qk, j * P:(j + 1) * P]
                        for src in (U, V):
                            mm = pe.matmul(o, src[:, qk, 2 * pair:2 * pair + 2, :].rearrange("p r d -> p (r d)"),
                                           EYE[:, :], is_transpose=True, start=(src is U), stop=(src is V),
                                           skip_group_check=True)
                mm.then_inc(done, 1)

            def step(p, i, c, v2, do_a, do_b, do_c, first):
                q = 1 - p
                if do_a:
                    pe.wait_ge(xs_ready, c(1))
                    if not isinstance(i, int) or i >= 1:
                        pe.wait_ge(v_evac, c(0))
                    project(0, p, raw_q)
                if do_b:
                    pe.wait_ge(u_ready, c(0))
                    pe.wait_ge(vv_ready, c(0))
                    if do_c:
                        pe.wait_ge(xb_ready, c(-1))
                    turn(0, q, t0_ready)
                if do_a:
                    pe.wait_ge(sq_q, c(1))
                    project(1, p, raw_k)
                if do_b:
                    pe.wait_ge(tev0, c(0))
                    turn(1, q, t1_ready)
                if do_a:
                    pe.wait_ge(sq_k, c(1))
                    project(2, p, raw_v)
                if do_b:
                    pe.wait_ge(tev1, c(0))
                    pe.wait_ge(halo_ready, c(0))
                    if do_c:
                        pe.wait_ge(sm_ready, c(-1))
                    for r in range(2):
                        pe.matmul(PS[:, SB + r, :], EYEB[:, :],
                                  rep(MASK[:, 1 if first else 0, :], [P, NP_, 2 * WIN], 1),
                                  start=True, stop=False, skip_group_check=True)
                    for j in range(NP_):
                        for w in range(NW):
                            for r in range(2):
                                mm = pe.matmul(PS[WIN * w:WIN * (w + 1), SB + r, j * 2 * WIN:(j + 1) * 2 * WIN],
                                               QT[DH * r:DH * (r + 1), q, j, WIN * w:WIN * (w + 1)],
                                               KT[DH * r:DH * (r + 1), q, j, WIN * w:WIN * (w + 2)],
                                               start=False, stop=True, skip_group_check=True)
                    mm.then_inc(s_ready, 1)
                if do_c:
                    pe.wait_ge(v2_odd if p else v2_even, v2(0))
                    pe.wait_ge(p_ready, c(0))
                    if not do_b:
                        pe.wait_ge(xb_ready, c(-1))
                    for j in range(NP_):
                        mm = pe.matmul(PS[:, TQ + j // 4, (j % 4) * P:(j % 4 + 1) * P],
                                       PR[:, 2 * j:2 * j + 2, :].rearrange("p r k -> p (r k)"),
                                       EYE[:, :], is_transpose=True, start=True, stop=True,
                                       skip_group_check=True)
                    mm.then_inc(pt_ready, 1)
                    pe.wait_ge(init, 5)
                    pe.wait_ge(ptev, c(-1))
                    pe.wait_ge(otev, c(-1))
                    for j in range(NP_):
                        for w in range(NW):
                            for r in range(2):
                                half = DH * (j % 2)
                                at = (j // 2) * P + WIN * w
                                mm = pe.matmul(PS[half:half + DH, OB + r, at:at + WIN],
                                               V2[DH * r:DH * (r + 1), p, w, j * DH:(j + 1) * DH],
                                               PT[DH * r:DH * (r + 1), j, WIN * w:WIN * (w + 1)],
                                               start=True, stop=True, skip_group_check=True)
                    mm.then_inc(o_ready, 1)
                    pe.wait_ge(otev, c(0))
                    for h in range(NP_):
                        mm = pe.matmul(PS[:, TQ, 0:P], WO[:, h, :], OT[:, h, :], start=(h == 0), stop=(h == NP_ - 1))
                    mm.then_inc(wo_ready, 1)

            def ffn(inv, lay):
                L = pe.snap(lay * 4 + (lncount(inv) + 0))
                G = pe.snap(lay * 4 + inv * DEPTH * 4)
                G3 = pe.snap(lay * 12 + inv * DEPTH * 12)
                pe.wait_ge(ffn_w, pe.snap(lay * (16 * F_DMAS) + (inv * DEPTH + 1) * 16 * F_DMAS))

                def xf(g):
                    return pe.snap(G + g + 1)
                ln_center(pe.snap(L + 0), XF[:, :], xf_ready, xf(0))
                ln_var(pe.snap(L + 0))
                ln_spread(pe.snap(L + 0))
                for g in range(NG):
                    more = g + 1 < NG
                    v = pe.snap(L + (g + 1))
                    if more:
                        ln_center(v, XF[:, :], xf_ready, xf(g + 1))
                    pe.wait_ge(ln_done, v)
                    for t in range(6):
                        gate, n = t < 3, t % 3
                        if t == 3 and more:
                            ln_var(v)
                        if g == 0 and t < 4:
                            pass
                        elif t in (1, 2):
                            pe.wait_ge(ht_ready, pe.snap(G3 + (3 * g - 3 + t)))
                        elif t == 0:
                            pe.wait_ge(gelu_ready, pe.snap(G3 + 3 * g))
                        elif t == 3:
                            pe.wait_ge(ht_ready, pe.snap(G3 + 3 * g))
                        else:
                            pe.wait_ge(gelu_ready, pe.snap(G3 + (3 * g + t - 3)))
                        at, rows = FT[n]
                        at += DI if gate else 0
                        pe.matmul(PS[0:rows, HB + (6 * g + t) % 4, :], W1[:, at:at + rows], XN[:, g % 2, :],
                                  start=True, stop=True).then_inc(h_ready, 1)
                    if more:
                        ln_spread(v)
                    pe.wait_ge(ht_ready, pe.snap(G3 + (3 * g + 3)))
                    if g > 0:
                        pe.wait_ge(xa_ready, pe.snap(G + (g + 4 + 4 * inv)))
                    for n, (_, rows) in enumerate(FT):
                        mm = pe.matmul(PS[:, YB, :], W2[0:rows, n, :], HT[0:rows, n, :], start=(n == 0), stop=(n == 2))
                    mm.then_inc(y_ready, 1)

            stack = layers(pe, step, attn_start, ffn)

            def norm_in(inv):
                for g in range(NG):
                    v = 0 if inv == 0 else lncount(1) - 4
                    ready, value = (xr_ready, NG) if inv == 0 else (xr_mid, NG)
                    r = XR[:, g * GT:(g + 1) * GT]
                    ln_center(v + g, r, ready, value, prev=v + g > 0)
                    ln_var(v + g, prev=v + g > 0)
                    ln_spread(v + g, prev=v + g > 0)

            norm_in(0)
            stack(0)

            pe.wait_ge(mid_w, 16 * 6)
            v0 = 4 + 4 * DEPTH
            for g in range(NG):
                ln(v0 + 2 * g, XR[:, g * GT:(g + 1) * GT], xr_half, NG)
                ln(v0 + 2 * g + 1, XB[:, 1 + g * GT:1 + (g + 1) * GT], ln_done, v0 + 2 * g + 1)
                pe.wait_ge(ln_done, v0 + 2 * g + 2)
                if g > 0:
                    pe.wait_ge(mq_done, g)
                pe.matmul(PS[:, 3, :], WQM[:, :], XN[:, 0, :], start=True, stop=True).then_inc(mq_ready, 1)
                if g > 0:
                    pe.wait_ge(k4_ready, g)
                    pe.wait_ge(vx_ready, g)
                for j in range(4):
                    mm = pe.matmul(PS[:, 4 + j // 2, (j % 2) * 256:(j % 2 + 1) * 256], XN[:, 0, j * P:(j + 1) * P],
                                   WKVM[:, :], start=True, stop=True)
                mm.then_inc(mkv_ready, 1)
                pe.wait_ge(k4_ready, g + 1)
                pe.wait_ge(vx_ready, g + 1)
                for j in range(4):
                    mm = pe.matmul(PS[:, 7, 0:P + 1], K4[:, j, :], VX[:, j, :], start=(g == 0 and j == 0),
                                   stop=(g == NG - 1 and j == 3))
                mm.then_inc(kv_ready, 1)
            pe.wait_ge(kvm_ready, 1)
            for g in range(NG):
                q = QB[:, g * GT:(g + 1) * GT]
                if g == 0:
                    pe.wait_ge(mq_done, NG)
                else:
                    pe.wait_ge(mg_ready, g)
                pe.matmul(PS[:, 3, :], KVM, q, start=True, stop=True)
                pe.matmul(PS[:, 4, :], KSM, q, start=True, stop=True).then_inc(num_ready, 1)
                pe.wait_ge(ao_ready, g + 1)
                pe.matmul(PS[:, 5, :], PROJ[:, :], EL, start=True, stop=True).then_inc(proj_ready, 1)
                v = v0 + 2 * NG + g
                ln(v, XB[:, 1 + g * GT:1 + (g + 1) * GT], x1_ready, g + 1)
                pe.wait_ge(ln_done, v + 1)
                for n in range(4):
                    mm = pe.matmul(PS[:, 3 + n, :], FC1[:, n * P:(n + 1) * P], XN[:, 0, :], start=True, stop=True)
                mm.then_inc(mh_ready, 1)
                pe.wait_ge(mg_ready, g + 1)
                if g > 0:
                    pe.wait_ge(xr_mid, g)
                for n in range(4):
                    mm = pe.matmul(PS[:, 7, :], FC2[:, n, :], HT[:, n, :], start=(n == 0), stop=(n == 3))
                mm.then_inc(my_ready, 1)

            norm_in(1)
            stack(1)

            pe.wait_ge(xr_half, 2 * NG)
            for c in range(CH):
                mm = pe.transpose(PS[:, c // 4, (c % 4) * P:(c % 4 + 1) * P], XR[:, c * P:(c + 1) * P], EYE[:, :])
                if c % 4 == 3:
                    mm.then_inc(o_t, 1)

        @block.scalar
        def _(act):
            def ln(v, scale, prev=True):
                act.wait_ge(cen_ready, act.snap(v + 1) if not isinstance(v, int) else v + 1)
                act.activation(D2, PS[:, CEN, :], ACT.Square).then_inc(d2_ready, 1)
                if prev:
                    act.wait_ge(ln_done, v)
                act.activation(DG, PS[:, CEN, :], ACT.Copy, scale=scale).then_inc(dg_ready, 1)

            act.wait_ge(consts, 16 * 6)
            act.activation(MASK[:, :, :], MASKF[:, :, :], ACT.Copy)
            act.activation(EYEB[:, :], EYE[:, :], ACT.Copy).then_inc(cast, 1)
            for b in range(4):
                act.wait_ge(xt_ready, b + 1)
                act.activation(XR[:, b * GT:(b + 1) * GT], PS[:, b, :], ACT.Copy).then_inc(xr_ready, 1)

            def attn_start(inv, lay):
                act.wait_ge(init, 5)
                act.wait_ge(xa_ready, act.snap(lay * 4 + (inv * DEPTH * 4 + 4 + 4 * inv)))

            def step(p, i, c, v2, do_a, do_b, do_c, first):
                q = 1 - p
                if do_a:
                    if not isinstance(i, int):
                        act.wait_ge(raw_v, c(-1))
                    at = i * P
                    act.activation(XS[0:DH, p, :], XA[0:DH, bass.ds(at + 1, P)], ACT.Copy)
                    act.activation(XS[DH:P, p, :], XA[DH:P, bass.ds(at, P)], ACT.Copy).then_inc(xs_ready, 1)
                    act.wait_ge(raw_q, c(1))
                    if not isinstance(i, int) or i >= 1:
                        act.wait_ge(qn_ready, c(0))
                    src = PS[:, RAW:RAW + 2, :]
                    act.activation(RAWQK[:, 0].rearrange("p (b h) d -> p b (h d)", b=2), src, ACT.Copy)
                    act.activation(SQ[:, 0].rearrange("p (b h) d -> p b (h d)", b=2), src, ACT.Square).then_inc(sq_q, 1)

                def evac(g, ready, done):
                    act.wait_ge(ready, c(0))
                    act.activation(QT[:, q, 4 * g:4 * g + 4, :], PS[:, TQ, :].rearrange("p (j t) -> p j t", t=P), ACT.Copy)
                    act.activation(KT[:, q, 4 * g:4 * g + 4, WIN:], PS[:, TK, :].rearrange("p (j t) -> p j t", t=P),
                                   ACT.Copy).then_inc(done, 1)
                if do_b:
                    evac(0, t0_ready, tev0)
                if do_a:
                    act.wait_ge(raw_k, c(1))
                    act.activation(RAWQK[:, 1].rearrange("p (b h) d -> p b (h d)", b=2), src, ACT.Copy)
                    act.activation(SQ[:, 1].rearrange("p (b h) d -> p b (h d)", b=2), src, ACT.Square).then_inc(sq_k, 1)
                if do_b:
                    evac(1, t1_ready, tev1)
                    act.wait_ge(tev1, c(0))
                    act.activation(KT[:, p, :, 0:WIN], KT[:, q, :, P:P + WIN], ACT.Copy,
                                   scale=NEXT[:, :]).then_inc(halo_ready, 1)
                if do_a:
                    act.wait_ge(raw_v, c(1))
                    if not isinstance(i, int):
                        act.wait_ge(v2_odd if p else v2_even, v2(0))
                        act.wait_ge(v2_even if p else v2_odd, v2(p))
                    elif i == 1:
                        act.wait_ge(v2_even, v2(1))
                    act.activation(VS[:, p, :].rearrange("p (b t) -> p b t", b=2), src, ACT.Copy).then_inc(v_evac, 1)
                if do_c:
                    act.wait_ge(pt_ready, c(0))
                    act.activation(PT[:, :, :].rearrange("p (b j) t -> p b (j t)", b=2), PS[:, TQ:TQ + 2, :],
                                   ACT.Copy).then_inc(ptev, 1)
                if do_b:
                    act.wait_ge(sm_ready, c(0))
                    act.activation(SM[:, q], SM[:, q], ACT.Exp, scale=QK_SCALE).then_inc(e_ready, 1)
                if do_c:
                    act.wait_ge(o_ready, c(1))
                    act.activation(OT[:, :, :].rearrange("p (b j) t -> p b (j t)", b=2), PS[:, OB:OB + 2, :],
                                   ACT.Copy).then_inc(otev, 1)

            def ffn(inv, lay):
                L = act.snap(lay * 4 + lncount(inv))
                G3 = act.snap(lay * 12 + inv * DEPTH * 12)
                H6 = act.snap(lay * 24 + inv * DEPTH * 24)
                act.wait_ge(ffn_w, act.snap(lay * (16 * F_DMAS) + (inv * DEPTH + 1) * 16 * F_DMAS))

                def shifted(g):
                    if g > 0:
                        act.wait_ge(cen_ready, act.snap(L + g))
                    at = g * GT
                    act.activation(XF[0:DH, :], XB[0:DH, at + 1:at + 1 + GT], ACT.Copy)
                    act.activation(XF[DH:P, :], XB[DH:P, at:at + GT], ACT.Copy).then_inc(xf_ready, 1)

                act.wait_ge(xb_ready, act.snap(lay * CH + ((inv * DEPTH + 1) * CH + 1)))
                shifted(0)
                ln(L, SMALL[:, S_G:S_G + 1])
                for g in range(NG):
                    if g + 1 < NG:
                        shifted(g + 1)
                        ln(act.snap(L + (g + 1)), SMALL[:, S_G:S_G + 1])
                    for n, (_, rows) in enumerate(FT):
                        act.wait_ge(h_ready, act.snap(H6 + (6 * g + n + 1)))
                        if g > 0:
                            act.wait_ge(ht_ready, act.snap(G3 + (3 * g - 2 + n)))
                        act.activation(GB[0:rows, n, :], PS[0:rows, HB + (6 * g + n) % 4, :], ACT.Gelu,
                                       bias=SMALL[0:rows, S_B1G + n:S_B1G + n + 1]).then_inc(gelu_ready, 1)

            stack = layers(act, step, attn_start, ffn)
            for g in range(NG):
                ln(g, 1.0, prev=g > 0)
            stack(0)

            act.wait_ge(mid_w, 16 * 6)
            v0 = 4 + 4 * DEPTH
            for g in range(NG):
                ln(v0 + 2 * g, 1.0)
                ln(v0 + 2 * g + 1, MSMALL[:, M_G1:M_G1 + 1])
                act.wait_ge(el_q, g + 1)
                act.activation(EL, EL, ACT.Exp).then_inc(ex_q, 1)
                act.wait_ge(mkv_ready, g + 1)
                if g > 0:
                    act.wait_ge(kv_ready, g)
                act.activation(VX[:, :, 0:P], PS[:, 4:6, :].rearrange("p b (j t) -> p (b j) t", j=2)[:, :, P:2 * P],
                               ACT.Copy).then_inc(vx_ready, 1)
                act.wait_ge(el_k, g + 1)
                act.activation(EL, EL, ACT.Exp).then_inc(ex_k, 1)
            for g in range(NG):
                ln(v0 + 2 * NG + g, MSMALL[:, M_G2:M_G2 + 1])
                act.wait_ge(mh_ready, g + 1)
                if g > 0:
                    act.wait_ge(my_ready, g)
                for n in range(4):
                    ins = act.activation(HT[:, n, :], PS[:, 3 + n, :], ACT.Gelu,
                                         bias=MSMALL[:, M_FC1B + n:M_FC1B + n + 1])
                ins.then_inc(mg_ready, 1)
            for g in range(NG):
                ln(lncount(1) - 4 + g, 1.0)
            stack(1)
            for b in range(4):
                act.wait_ge(o_t, b + 1)
                act.activation(XIO[:, 4 * b:4 * b + 4, :], PS[:, b, :].rearrange("p (c d) -> p c d", d=P),
                               ACT.Copy).then_inc(o_c, 1)

        @block.vector
        def _(dve):
            dve.memset(ONES[:, :], 1.0).then_inc(init, 1)
            dve.memset(MEAN[:, :], 1.0 / P).then_inc(init, 1)
            dve.memset(XA[:, 0:1], 0.0).then_inc(init, 1)
            dve.memset(XB[:, 0:1], 0.0).then_inc(init, 1)
            dve.memset(VX[:, :, P:P + 1], 1.0).then_inc(init, 1)
            dve.memset(VS[:, 1, :], 0.0).then_inc(o_ready, 2)
            dve.memset(KT[:, 0, :, 0:WIN], 0.0).then_inc(halo_ready, 1)
            for started in (p_ready, pt_ready, otev, xb_ready):
                dve.engine_nop().then_inc(started, 1)

            def rsqrt(y, x, half, u, eps, eps_op):
                dve.tensor_scalar(x, x, eps, None, eps_op)
                dve.drain()
                dve.tensor_scalar(half, x, -0.5, None, ALU.mult)
                dve.tensor_scalar(u.bitcast(I32), x.bitcast(I32), 1, None, ALU.logical_shift_right)
                dve.drain()
                dve.tensor_scalar(y.bitcast(I32), u.bitcast(I32), -1.0, RSQRT_MAGIC, ALU.mult, ALU.add)
                for n in range(3):
                    dve.drain()
                    dve.tensor_tensor(u, y, half, ALU.mult)
                    dve.drain()
                    dve.tensor_tensor(u, u, y, ALU.mult)
                    dve.drain()
                    last = dve.scalar_tensor_tensor(y, u, 1.5, y, ALU.add, ALU.mult)
                return last

            def value(v, k):
                return v + k if isinstance(v, int) else dve.snap(v + k)

            def ln_rstd(v):
                dve.wait_ge(var_ready, value(v, 1))
                dve.tensor_copy(V4[:, :], PS[:, VAR, 0:4])
                dve.drain()
                rsqrt(R4[:, :], V4[:, :], NX4[:, :], NU4[:, :], EPS, ALU.add).then_inc(r4_ready, 1)
                dve.drain()

            def ln_diag(v, prev=True):
                if prev:
                    dve.wait_ge(rb_ready, v)
                for j in range(4):
                    ins = dve.tensor_scalar(DIAG[:, j * P:(j + 1) * P], EYE[:, :], R4[:, j:j + 1], None, ALU.mult)
                ins.then_inc(diag_ready, 1)

            def ln_apply(v, o, bias=None, done=None):
                dve.wait_ge(rb_ready, value(v, 1))
                dve.wait_ge(dg_ready, value(v, 1))
                ins = dve.tensor_tensor(o, DG, PS[:, RB, :], ALU.mult)
                if bias is not None:
                    dve.drain()
                    ins = dve.tensor_scalar(o, o, bias, None, ALU.add)
                ins.then_inc(ln_done, 1)
                if done is not None:
                    dve.engine_nop().then_inc(done, 1)

            def attn_start(inv, lay):
                pass

            def step(p, i, c, v2, do_a, do_b, do_c, first):
                q = 1 - p
                if do_a:
                    dve.wait_ge(sq_q, c(1))
                    dve.tensor_reduce(SS[:, 0:HEADS], SQ[:, 0], AX.X, ALU.add)
                    dve.wait_ge(sq_k, c(1))
                    dve.tensor_reduce(SS[:, HEADS:2 * HEADS], SQ[:, 1], AX.X, ALU.add)
                    dve.drain()
                    rsqrt(RN[:, :, :].rearrange("p a b -> p (a b)"), SS[:, :], NX[:, :], NU[:, :], 1e-24, ALU.max)
                    dve.drain()
                if do_b:
                    dve.wait_ge(s_ready, c(0))
                    sc = PS[:, SB:SB + 2, :].rearrange("p b (j k) -> p (b j) k", k=2 * WIN)
                    dve.tensor_reduce(MX[:, :], sc, AX.X, ALU.max)
                    dve.drain()
                    if not isinstance(i, int):
                        dve.wait_ge(p_ready, c(-1))
                    dve.tensor_tensor(SM[:, q], sc, rep(MX[:, :], [P, HEADS, 2 * WIN], 2),
                                      ALU.subtract).then_inc(sm_ready, 1)
                if do_a:
                    if not isinstance(i, int) or i >= 1:
                        dve.wait_ge(vv_ready, c(0))
                    for k in range(2):
                        ins = dve.tensor_tensor(QN[:, k], RAWQK[:, k], rep(RN[:, k, :], [P, HEADS, DH], 2), ALU.mult)
                    ins.then_inc(qn_ready, 1)
                    dve.drain()
                    dve.wait_ge(tab_ready, c(1))
                    if not isinstance(i, int) or i >= 1:
                        dve.wait_ge(t1_ready, c(0))
                    for k in range(2):
                        ins = dve.tensor_tensor(paired(U[:, k]), split(QN[:, k]),
                                                per_dim(TAB[:, 2 * k * DH:(2 * k + 1) * DH], DH), ALU.mult)
                    ins.then_inc(u_ready, 1)
                if do_b:
                    dve.wait_ge(e_ready, c(0))
                    dve.tensor_reduce(SUM[:, q, :], SM[:, q], AX.X, ALU.add)
                    dve.drain()
                    dve.reciprocal(SUM[:, q, :], SUM[:, q, :]).then_inc(rs_ready, 1)
                if do_c:
                    dve.wait_ge(wo_ready, c(-1))
                    at = (i - 2) * P + 1
                    dve.tensor_tensor(XB[:, bass.ds(at, P)], PS[:, TQ, 0:P], XA[:, bass.ds(at, P)],
                                      ALU.add).then_inc(xb_ready, 1)

            def ffn(inv, lay):
                L = dve.snap(lay * 4 + lncount(inv))
                G = dve.snap(lay * 4 + inv * DEPTH * 4)
                G3 = dve.snap(lay * 12 + inv * DEPTH * 12)
                H6 = dve.snap(lay * 24 + inv * DEPTH * 24)
                dve.wait_ge(ffn_w, dve.snap(lay * (16 * F_DMAS) + (inv * DEPTH + 1) * 16 * F_DMAS))
                ln_rstd(L)
                ln_diag(L)
                ln_apply(L, XN[:, 0, :], SMALL[:, S_B:S_B + 1])
                for g in range(NG):
                    v = dve.snap(L + (g + 1))
                    if g + 1 < NG:
                        ln_rstd(v)
                        ln_diag(v)
                    for n, (_, rows) in enumerate(FT):
                        dve.wait_ge(h_ready, dve.snap(H6 + (6 * g + n + 4)))
                        dve.wait_ge(gelu_ready, dve.snap(G3 + (3 * g + n + 1)))
                        if g > 0:
                            dve.wait_ge(y_ready, dve.snap(G + g))
                        dve.scalar_tensor_tensor(HT[0:rows, n, :], PS[0:rows, HB + (6 * g + n + 3) % 4, :],
                                                 SMALL[0:rows, S_B1A + n:S_B1A + n + 1], GB[0:rows, n, :],
                                                 ALU.add, ALU.mult).then_inc(ht_ready, 1)
                    if g + 1 < NG:
                        ln_apply(v, XN[:, (g + 1) % 2, :], SMALL[:, S_B:S_B + 1])
                    dve.wait_ge(y_ready, dve.snap(G + (g + 1)))
                    s = slice(1 + g * GT, 1 + (g + 1) * GT)
                    dve.scalar_tensor_tensor(XA[:, s], PS[:, YB, :], SMALL[:, S_B2:S_B2 + 1], XB[:, s],
                                             ALU.add, ALU.add).then_inc(xa_ready, 1)

            stack = layers(dve, step, attn_start, ffn)

            def norm_in(v, inv):
                for g in range(NG):
                    ln_rstd(v + g)
                    ln_diag(v + g, prev=v + g > 0)
                    ln_apply(v + g, XA[:, 1 + g * GT:1 + (g + 1) * GT], done=xa_ready)

            def add_half():
                for g in range(NG):
                    r = XR[:, g * GT:(g + 1) * GT]
                    dve.scalar_tensor_tensor(r, XA[:, 1 + g * GT:1 + (g + 1) * GT], 0.5, r,
                                             ALU.mult, ALU.add).then_inc(xr_half, 1)

            norm_in(0, 0)
            stack(0)
            dve.drain()
            add_half()

            dve.wait_ge(consts, 16 * 6)
            dve.wait_ge(mid_w, 16 * 6)
            v0 = 4 + 4 * DEPTH
            for g in range(NG):
                s = slice(1 + g * GT, 1 + (g + 1) * GT)
                ln_rstd(v0 + 2 * g)
                ln_diag(v0 + 2 * g)
                ln_apply(v0 + 2 * g, XB[:, s])
                ln_rstd(v0 + 2 * g + 1)
                ln_diag(v0 + 2 * g + 1)
                ln_apply(v0 + 2 * g + 1, XN[:, 0, :], MSMALL[:, M_B1:M_B1 + 1])
                dve.wait_ge(mq_ready, g + 1)
                dve.tensor_scalar(EL, PS[:, 3, :], 0.0, None, ALU.min).then_inc(el_q, 1)
                dve.wait_ge(ex_q, g + 1)
                dve.scalar_tensor_tensor(QB[:, g * GT:(g + 1) * GT], PS[:, 3, :], 0.0, EL, ALU.max,
                                         ALU.add).then_inc(mq_done, 1)
                dve.drain()
                dve.wait_ge(mkv_ready, g + 1)
                keys = PS[:, 4:6, :].rearrange("p b (j t) -> p (b j) t", j=2)[:, :, 0:P]
                ek = EL.rearrange("p (j t) -> p j t", t=P)
                dve.wait_ge(vx_ready, g + 1)
                dve.tensor_scalar(ek, keys, 0.0, None, ALU.min).then_inc(el_k, 1)
                dve.wait_ge(ex_k, g + 1)
                if g > 0:
                    dve.wait_ge(kv_ready, g)
                dve.scalar_tensor_tensor(K4, keys, 0.0, ek, ALU.max, ALU.add).then_inc(k4_ready, 1)
                dve.drain()
            dve.wait_ge(kv_ready, NG)
            dve.tensor_copy(KS1[:, :], PS[:, 7, P:P + 1])
            dve.tensor_tensor(KVM, PS[:, 7, 0:P], BLOCKS[:, :], ALU.mult)
            dve.drain()
            dve.tensor_scalar(KSM, BLOCKS[:, :], KS1[:, :], None, ALU.mult).then_inc(kvm_ready, 1)
            for g in range(NG):
                s = slice(1 + g * GT, 1 + (g + 1) * GT)
                den = XF[:, :]
                dve.wait_ge(num_ready, g + 1)
                dve.tensor_scalar(den, PS[:, 4, :], 1e-6, None, ALU.add)
                dve.drain()
                dve.reciprocal(den, den)
                dve.drain()
                dve.tensor_tensor(EL, PS[:, 3, :], den, ALU.mult).then_inc(ao_ready, 1)
                dve.wait_ge(proj_ready, g + 1)
                dve.scalar_tensor_tensor(XB[:, s], PS[:, 5, :], MSMALL[:, M_PB:M_PB + 1], XB[:, s], ALU.add,
                                         ALU.add).then_inc(x1_ready, 1)
                v = v0 + 2 * NG + g
                ln_rstd(v)
                ln_diag(v)
                ln_apply(v, XN[:, 0, :], MSMALL[:, M_B2:M_B2 + 1])
                dve.wait_ge(my_ready, g + 1)
                dve.scalar_tensor_tensor(XB[:, s], PS[:, 7, :], MSMALL[:, M_FC2B:M_FC2B + 1], XB[:, s], ALU.add, ALU.add)
                dve.drain()
                r = XR[:, g * GT:(g + 1) * GT]
                dve.tensor_tensor(r, r, XB[:, s], ALU.add).then_inc(xr_mid, 1)
            norm_in(lncount(1) - 4, 1)
            stack(1)
            dve.drain()
            add_half()

        @block.gpsimd
        def _(pool):
            pool.wait_ge(consts, 16 * 6)

            def attn_start(inv, lay):
                pool.wait_ge(attn_w, pool.snap(lay * (16 * A_DMAS) + (inv * DEPTH + 1) * 16 * A_DMAS))

            def step(p, i, c, v2, do_a, do_b, do_c, first):
                if do_a:
                    if not isinstance(i, int) or i >= 1:
                        pool.wait_ge(u_ready, c(0))
                        pool.wait_ge(vv_ready, c(0))
                    rot = ROT[:, bass.ds(i, 1), :].rearrange("p a b -> p (a b)")
                    pool.tensor_tensor(TAB[:, :], rot, QKS[:, :], ALU.mult).then_inc(tab_ready, 1)
                if do_c:
                    pool.wait_ge(rs_ready, c(-1))
                    pool.wait_ge(pt_ready, c(-1))
                    pool.tensor_tensor(paired(PR[:, :, :]), split(SM[:, p]),
                                       split(SUM[:, p, :].unsqueeze(2)).broadcast_to([P, 2, NP_, 2 * WIN]),
                                       ALU.mult).then_inc(p_ready, 1)
                if do_a:
                    pool.wait_ge(tab_ready, c(1))
                    pool.wait_ge(qn_ready, c(1))
                    if not isinstance(i, int) or i >= 1:
                        pool.wait_ge(t1_ready, c(0))
                    half = DH // 2
                    for k in range(2):
                        for h in range(2):
                            t = TAB[:, (2 * k + 1) * DH + h * half:(2 * k + 1) * DH + (h + 1) * half]
                            ins = pool.tensor_tensor(paired(V[:, k])[:, :, :, h * half:(h + 1) * half],
                                                     split(QN[:, k])[:, :, :, (1 - h) * half:(2 - h) * half],
                                                     per_dim(t, half), ALU.mult)
                    ins.then_inc(vv_ready, 1)

            def ffn(inv, lay):
                pass

            stack = layers(pool, step, attn_start, ffn)
            stack(0)
            stack(1)

        @block.sync
        def _(sp):
            for t, n in ((EYE, "c_eye"), (CENTER, "c_center"), (BLOCKS, "c_blocks"), (NEXT, "c_next")):
                sp.dma_start(t[:, :], a[n]).then_inc(consts, 16)
            sp.dma_start(MASKF[:, :, :].rearrange("p a b -> p (a b)"), a["c_masks"]).then_inc(consts, 16)
            sp.dma_start(XIO, a["x"].rearrange("b (c p) d -> p (b c) d", p=P)).then_inc(x_in, 16)
            sp.dma_start(ROT[:, :, :].rearrange("p a b -> p (a b)"), a["c_rot"]).then_inc(consts, 16)

            def load_attn(lay):
                sp.dma_start(WQKV[:, :], a["wqkv"][bass.ds(lay, 1)].rearrange("l p n -> p (l n)")).then_inc(attn_w, 16)
                sp.dma_start(WO[:, :, :], a["wo"][bass.ds(lay, 1)].rearrange("l (h p) n -> p (l h) n", p=P)).then_inc(attn_w, 16)
                sp.dma_start(QKS[:, :], a["qks"][bass.ds(lay, 1), :].broadcast_to([P, 4 * DH])).then_inc(attn_w, 16)

            def load_ffn(lay):
                sp.dma_start(W1[:, :], a["w1"][bass.ds(lay, 1)].rearrange("l p n -> p (l n)")).then_inc(ffn_w, 16)
                sp.dma_start(W2[0:FT[0][1], 0:2, :],
                             a["w2"][bass.ds(lay, 1), 0:FT[2][0]].rearrange("l (i p) n -> p (l i) n", i=2)).then_inc(ffn_w, 16)
                sp.dma_start(W2[0:FT[2][1], 2, :],
                             a["w2"][bass.ds(lay, 1), FT[2][0]:DI].rearrange("l p n -> p (l n)")).then_inc(ffn_w, 16)
                sp.dma_start(SMALL[:, :], a["small"][bass.ds(lay, 1)].rearrange("l p n -> p (l n)")).then_inc(ffn_w, 16)

            load_attn(0)
            for t, n in ((WQM, "m_q"), (WKVM, "m_kv"), (PROJ, "m_proj"), (FC1, "m_fc1"), (MSMALL, "m_small")):
                sp.dma_start(t[:, :], a[n]).then_inc(mid_w, 16)
            sp.dma_start(FC2[:, :, :], a["m_fc2"].rearrange("(n p) d -> p n d", p=P)).then_inc(mid_w, 16)

            def attn_start(inv, lay):
                sp.wait_ge(init, 5)
                if inv == 0:
                    sp.wait_ge(xa_ready, sp.snap(lay * 4 + 4))
                else:
                    sp.wait_ge(xa_ready, sp.snap(lay * 4 + (DEPTH * 4 + 8)))
                load_ffn(lay)

            def step(p, i, c, v2, do_a, do_b, do_c, first):
                if not do_a:
                    return
                done = v2_odd if p else v2_even
                sp.wait_ge(v_evac, c(1))
                sp.wait_ge(o_ready, c(1))
                for r in range(2):
                    cols = slice(r * 512, (r + 1) * 512)
                    for w in range(NW):
                        own = VS[WIN * w:WIN * (w + 1), p, cols]
                        before = VS[WIN * (w - 1):WIN * w, p, cols] if w else VS[P - WIN:P, 1 - p, cols]
                        sp.dma_start(V2[DH * r:DH * r + WIN, p, w, :], before).then_inc(done, 16)
                        sp.dma_start(V2[DH * r + WIN:DH * (r + 1), p, w, :], own).then_inc(done, 16)

            def ffn(inv, lay):
                sp.wait_ge(init, 5)
                sp.wait_ge(xb_ready, sp.snap(lay * CH + ((inv * DEPTH + 1) * CH + 1)))
                load_attn(lay + 1)

            sp.wait_ge(init, 5)
            sp.wait_ge(halo_ready, 1)
            stack = layers(sp, step, attn_start, ffn)
            stack(0)
            stack(1)
            sp.wait_ge(attn_w, 16 * A_DMAS * (2 * DEPTH + 1))
            for b in range(4):
                sp.wait_ge(o_c, b + 1)
                sp.dma_start(out.rearrange("b (c p) d -> p (b c) d", p=P)[:, 4 * b:4 * b + 4, :],
                             XIO[:, 4 * b:4 * b + 4, :]).then_inc(stored, 16)
            sp.wait_ge(stored, 16 * 4)


def kernel(**inputs):
    import concourse.bacc as bacc
    from concourse.bass_utils import run_bass_kernel_spmd

    def get(name):
        return np.ascontiguousarray(inputs[name])

    def again(w):
        return np.concatenate([w, w[:1]], 0)

    def swapped(w):
        return np.concatenate([w[:, DH // 2:], w[:, :DH // 2]], 1)

    def tiles(v):
        cols = np.zeros((v.shape[0], P, 3), v.dtype)
        for n, (at, rows) in enumerate(FT):
            cols[:, :rows, n] = v[:, at:at + rows]
        return cols

    b1 = get("L0_ffn_b1")
    qs, ks = get("L0_ffn_q_scale"), get("L0_ffn_k_scale")
    small = np.concatenate([get("L0_ffn_ln_g")[:, :, None], get("L0_ffn_ln_b")[:, :, None],
                            get("L0_ffn_b2")[:, :, None], tiles(b1[:, :DI]), tiles(b1[:, DI:])], 2)
    mid = np.concatenate([get(n).reshape(P, 1) for n in (
        "L0_attn_norm1_g", "L0_attn_norm1_b", "L0_attn_proj_b", "L0_attn_norm2_g", "L0_attn_norm2_b",
        "L0_attn_fc2_b")] + [get("L0_attn_fc1_b").reshape(4, P).T], 1)
    arrays = {
        "x": get("L0_attn_x"),
        "wqkv": again(get("L0_ffn_Wqkv")), "wo": again(get("L0_ffn_Wo")),
        "qks": again(np.concatenate([qs, swapped(qs), ks, swapped(ks)], 1)),
        "w1": get("L0_ffn_W1"), "w2": get("L0_ffn_W2"), "small": small,
        "m_q": get("L0_attn_qkv_w")[:P].T, "m_kv": get("L0_attn_qkv_w")[P:].T,
        "m_proj": get("L0_attn_proj_w").T, "m_fc1": get("L0_attn_fc1_w").T, "m_fc2": get("L0_attn_fc2_w").T,
        "m_small": mid, **shape_constants(),
    }
    arrays = {n: np.ascontiguousarray(v) for n, v in arrays.items()}
    nc = bacc.Bacc("TRN2", target_bir_lowering=False, num_devices=1)
    aps = {n: nc.dram_tensor(n, v.shape, mybir.dt.from_np(v.dtype), kind="ExternalInput").ap() for n, v in arrays.items()}
    out = nc.dram_tensor("out", (1, NTOK, P), F32, kind="ExternalOutput").ap()
    build(nc, aps, out)
    got = run_bass_kernel_spmd(nc, [arrays], core_ids=[0])
    return got.results[0]["out"]
```

```python
from contextlib import ExitStack

import numpy as np

import concourse.bass as bass
from concourse import mybir

F32 = mybir.dt.float32
BF16 = mybir.dt.bfloat16
I32 = mybir.dt.int32
ALU = mybir.AluOpType
ACT = mybir.ActivationFunctionType
AX = mybir.AxisListType

P = 128
NTOK = 2048
CH = 16
GT = 512
NG = NTOK // GT
DEPTH = 6
HEADS = 16
DH = 64
NP_ = HEADS // 2
WIN = 32
NW = P // WIN
DI = 341
FT = [(0, 114), (114, 114), (228, 113)]
MH = 8
EPS = 1e-5
QK_SCALE = 8.0
MASKED = -1.0e30
RSQRT_MAGIC = float(0x5F3759DF)

RAW, TQ, TK, SB, OB = 0, 2, 3, 4, 6
CEN, VAR, RB, HB, YB = 0, 1, 2, 3, 7

S_G, S_B, S_B2, S_B1A, S_B1G, NSMALL = 0, 1, 2, 3, 6, 9
M_G1, M_B1, M_PB, M_G2, M_B2, M_FC2B, M_FC1B, NMSMALL = 0, 1, 2, 3, 4, 5, 6, 10


def shape_constants():
    half = np.arange(0, DH, 2, dtype=np.float32)
    inv_freq = (1.0 / np.float32(10000.0) ** (half / np.float32(DH))).astype(np.float32)
    tok = np.arange(NTOK, dtype=np.float32)
    freqs = (tok[:, None] * inv_freq[None, :]).astype(np.float32).astype(np.float64)
    base = ((half + np.float32(0.4 * DH)) / np.float32(1.4 * DH)).astype(np.float32).astype(np.float64)
    power = (np.arange(NTOK) % P) / (WIN // 2)
    scale = base[None, :] ** power[:, None]
    cos, sin = np.cos(freqs), np.sin(freqs)
    rot = np.concatenate(
        [np.concatenate([cos, cos, -sin, sin], 1) * np.tile(s, 4) for s in (scale, 1.0 / scale)], 1)
    rot = rot.astype(np.float32).reshape(CH, P, 4 * DH).transpose(1, 0, 2)
    to_next = np.tile(base ** (P / (WIN // 2)), 4).astype(np.float32).reshape(P, 1)
    q, k = np.arange(P)[:, None] % WIN, np.arange(2 * WIN)[None, :]
    seen = (k - WIN <= q) & (q <= k)
    first = seen & ((k >= WIN) | (np.arange(P)[:, None] >= WIN))
    masks = np.stack([np.where(m, 0.0, MASKED) for m in (seen, first)], 1).astype(np.float32)
    blocks = (np.arange(P)[:, None] // MH == np.arange(P)[None, :] // MH).astype(np.float32)
    eye = np.eye(P, dtype=np.float32)
    return {
        "c_rot": np.ascontiguousarray(rot.reshape(P, CH * 4 * DH)),
        "c_next": to_next,
        "c_masks": np.ascontiguousarray(masks.reshape(P, 4 * WIN)),
        "c_blocks": blocks,
        "c_eye": eye,
        "c_center": (eye - np.float32(1.0 / P)).astype(np.float32),
    }


def build(nc, a, out):
    ctx = ExitStack()
    with ctx:
        def sb(name, shape, dt=F32):
            return ctx.enter_context(nc.sbuf_tensor(name, shape, dt))

        def sem(name):
            return ctx.enter_context(nc.semaphore(name))

        XR = sb("XR", [P, NTOK])
        XA = sb("XA", [P, NTOK + 1])
        XB = sb("XB", [P, NTOK + 1])
        ROT = sb("ROT", [P, CH, 4 * DH])
        NEXT = sb("NEXT", [P, 1])
        MASKF = sb("MASKF", [P, 2, 2 * WIN])
        MASK = sb("MASK", [P, 2, 2 * WIN], BF16)
        EYE = sb("EYE", [P, P])
        EYEB = sb("EYEB", [P, P], BF16)
        CENTER = sb("CENTER", [P, P])
        BLOCKS = sb("BLOCKS", [P, P])
        ONES = sb("ONES", [P, P])
        MEAN = sb("MEAN", [P, 1])
        WQKV = sb("WQKV", [P, 3 * HEADS * DH])
        WO = sb("WO", [P, NP_, P])
        QKS = sb("QKS", [P, 4 * DH])
        W1 = sb("W1", [P, 2 * DI])
        W2 = sb("W2", [P, 3, P])
        SMALL = sb("SMALL", [P, NSMALL])
        XS = sb("XS", [P, 2, P])
        RAWQK = sb("RAWQK", [P, 2, HEADS, DH])
        SQ = sb("SQ", [P, 2, HEADS, DH])
        SS = sb("SS", [P, 2 * HEADS])
        NX = sb("NX", [P, 2 * HEADS])
        NU = sb("NU", [P, 2 * HEADS])
        RN = sb("RN", [P, 2, HEADS])
        TAB = sb("TAB", [P, 4 * DH])
        QN = sb("QN", [P, 2, HEADS, DH])
        U = sb("U", [P, 2, HEADS, DH])
        V = sb("V", [P, 2, HEADS, DH])
        QT = sb("QT", [P, 2, NP_, P])
        KT = sb("KT", [P, 2, NP_, WIN + P])
        MX = sb("MX", [P, HEADS])
        SM = sb("SM", [P, HEADS, 2 * WIN])
        SUM = sb("SUM", [P, HEADS])
        PR = sb("PR", [P, HEADS, 2 * WIN])
        PT = sb("PT", [P, NP_, P])
        VS = sb("VS", [P, 2, HEADS * DH])
        V2 = sb("V2", [P, 2, NW, NP_ * DH])
        ON = sb("ON", [P, HEADS, DH])
        OT = sb("OT", [P, NP_, P])
        XF = sb("XF", [P, GT])
        D2 = QT[:, 0, 0:4, :].rearrange("p a b -> p (a b)")
        DG = QT[:, 0, 4:8, :].rearrange("p a b -> p (a b)")
        DIAG = QT[:, 1, 0:4, :].rearrange("p a b -> p (a b)")
        V4 = sb("V4", [P, 4])
        NX4 = sb("NX4", [P, 4])
        NU4 = sb("NU4", [P, 4])
        R4 = sb("R4", [P, 4])
        XN = sb("XN", [P, 2, GT])
        gb_ = U[:, :, :, :].rearrange("p a b c -> p (a b c)")
        ht_ = V[:, :, :, :].rearrange("p a b c -> p (a b c)")
        GB = gb_.rearrange("p (i t) -> p i t", t=GT)
        HT = ht_.rearrange("p (i t) -> p i t", t=GT)
        XIO = QN[:, :, :, :].rearrange("p a b c -> p (a b c)").rearrange("p (c d) -> p c d", d=P)
        WQ_M = QKS[:, 0:P]
        WQM = sb("WQM", [P, P])
        WKVM = sb("WKVM", [P, 2 * P])
        PROJ = sb("PROJ", [P, P])
        FC1 = sb("FC1", [P, 4 * P])
        FC2 = sb("FC2", [P, 4, P])
        MSMALL = sb("MSMALL", [P, NMSMALL])
        QB = RAWQK[:, :, :, :].rearrange("p a b c -> p (a b c)")
        EL = SQ[:, 0, :, :].rearrange("p a b -> p (a b)")[:, 0:GT]
        K4 = SM[:, :, :].rearrange("p a b -> p (a b)")[:, 0:GT].rearrange("p (j d) -> p j d", d=P)
        VX = sb("VX", [P, 4, P + 1])
        KVM = PR[:, 0:2, :].rearrange("p a b -> p (a b)")
        KSM = PR[:, 2:4, :].rearrange("p a b -> p (a b)")
        KS1 = sb("KS1", [P, 1])

        PS = ctx.enter_context(nc.psum_tensor("PS", [P, 8, 512], F32))

        consts = sem("consts"); init = sem("init"); cast = sem("cast")
        attn_w = sem("attn_w"); ffn_w = sem("ffn_w"); mid_w = sem("mid_w")
        xs_ready = sem("xs_ready"); tab_ready = sem("tab_ready")
        raw_q = sem("raw_q"); raw_k = sem("raw_k"); raw_v = sem("raw_v")
        sq_q = sem("sq_q"); sq_k = sem("sq_k"); v_evac = sem("v_evac")
        raw_v0 = sem("raw_v0"); v0_evac = sem("v0_evac")
        qn_ready = sem("qn_ready"); u_ready = sem("u_ready"); vv_ready = sem("vv_ready"); rot_ready = sem("rot_ready")
        t0_ready = sem("t0_ready"); t1_ready = sem("t1_ready")
        tev0 = sem("tev0"); tev1 = sem("tev1"); halo_ready = sem("halo_ready")
        s_ready = sem("s_ready"); sm_ready = sem("sm_ready"); e_ready = sem("e_ready")
        rs_ready = sem("rs_ready"); on_ready = sem("on_ready"); to_ready = sem("to_ready")
        pt_ready = sem("pt_ready"); ptev = sem("ptev")
        v2_even = sem("v2_even"); v2_odd = sem("v2_odd")
        o_ready = sem("o_ready"); otev = sem("otev"); wo_ready = sem("wo_ready"); xb_ready = sem("xb_ready")
        xa_ready = sem("xa_ready")
        xf_ready = sem("xf_ready"); cen_ready = sem("cen_ready"); d2_ready = sem("d2_ready")
        dg_ready = sem("dg_ready"); var_ready = sem("var_ready"); r4_ready = sem("r4_ready")
        diag_ready = sem("diag_ready"); rb_ready = sem("rb_ready"); ln_done = sem("ln_done")
        h_ready = sem("h_ready"); gelu_ready = sem("gelu_ready"); ht_ready = sem("ht_ready"); y_ready = sem("y_ready")
        x_in = sem("x_in"); xt_ready = sem("xt_ready"); xr_ready = sem("xr_ready")
        mq_ready = sem("mq_ready"); mkv_ready = sem("mkv_ready"); el_q = sem("el_q"); el_k = sem("el_k")
        ex_q = sem("ex_q"); ex_k = sem("ex_k"); mq_done = sem("mq_done"); k4_ready = sem("k4_ready")
        vx_ready = sem("vx_ready"); kv_ready = sem("kv_ready"); kvm_ready = sem("kvm_ready")
        num_ready = sem("num_ready"); ao_ready = sem("ao_ready"); proj_ready = sem("proj_ready")
        x1_ready = sem("x1_ready"); mh_ready = sem("mh_ready"); mg_ready = sem("mg_ready")
        my_ready = sem("my_ready"); xr_mid = sem("xr_mid"); xr_half = sem("xr_half")
        o_t = sem("o_t"); o_c = sem("o_c"); stored = sem("stored")

        def lncount(inv):
            return 4 if inv == 0 else 4 + 4 * DEPTH + 12 + 4

        A_DMAS, F_DMAS, V2_DMAS = 3, 4, 16
        V2_INC = 16 * V2_DMAS

        def split(ap):
            return ap.rearrange("p (r j) d -> p r j d", r=2)

        def paired(ap):
            return ap.rearrange("p (j r) d -> p r j d", r=2)

        def per_dim(ap, n):
            return ap.unsqueeze(1).unsqueeze(1).broadcast_to([P, 2, NP_, n])

        def rep(ap, shape, axis):
            return ap.unsqueeze(axis).broadcast_to(shape)

        def stages(i):
            if not isinstance(i, int):
                return True, True, True, True
            return i < CH, 1 <= i <= CH, 2 <= i <= CH + 1, 3 <= i <= CH + 2

        def past(i, n):
            return not isinstance(i, int) or i >= n

        block = ctx.enter_context(nc.Block())

        def layers(eng, attn_step, attn_start, ffn, layer_end=None):
            def stack(inv):
                with eng.Fori(0, DEPTH) as lay:
                    first = eng.snap(lay * CH + inv * DEPTH * CH)

                    def counter(start):
                        kept = {}

                        def count(k):
                            if k not in kept:
                                kept[k] = eng.snap(start + k)
                            return kept[k]
                        return count

                    def v2_at(pairs):
                        return eng.snap(lay * (CH // 2 * V2_INC) + (inv * DEPTH * CH // 2 + pairs) * V2_INC)

                    attn_start(inv, lay)
                    for i in range(4):
                        attn_step(i % 2, i, counter(first + i), lambda off, i=i: v2_at((i + off) // 2 + 1))
                    with eng.Fori(0, CH // 2 - 3) as j:
                        at = eng.snap(first + j * 2)
                        c = counter(at + 4)
                        v2j = eng.snap(lay * (CH // 2 * V2_INC) + j * V2_INC + (inv * DEPTH * CH // 2) * V2_INC)
                        for p in (0, 1):
                            attn_step(p, eng.snap(j * 2 + (4 + p)), lambda k, p=p: c(k + p),
                                      lambda off, p=p: eng.snap(v2j + ((4 + p + off) // 2 + 1) * V2_INC))
                    c = counter(first + CH)
                    for i in range(CH - 2, CH + 3):
                        attn_step(i % 2, i, lambda k, i=i: c(k + i - CH), lambda off, i=i: v2_at((i + off) // 2 + 1))
                    ffn(inv, lay)
            return stack

        @block.tensor
        def _(pe):
            pe.wait_ge(consts, 16 * 6)
            pe.wait_ge(init, 5)
            pe.wait_ge(cast, 1)
            pe.wait_ge(x_in, 16)
            for c in range(CH):
                mm = pe.transpose(PS[:, c // 4, (c % 4) * P:(c % 4 + 1) * P], XIO[:, c, :], EYE[:, :])
                if c % 4 == 3:
                    mm.then_inc(xt_ready, 1)

            def ln_center(v, rhs, ready, value, prev=True):
                pe.wait_ge(ready, value)
                if prev:
                    pe.wait_ge(dg_ready, v)
                pe.matmul(PS[:, CEN, :], CENTER[:, :], rhs, start=True, stop=True).then_inc(cen_ready, 1)

            def ln_var(v, prev=True):
                pe.wait_ge(d2_ready, v + 1)
                if prev:
                    pe.wait_ge(r4_ready, v)
                for j in range(4):
                    mm = pe.matmul(PS[:, VAR, j:j + 1], D2[:, j * P:(j + 1) * P], MEAN[:, :], start=True, stop=True)
                mm.then_inc(var_ready, 1)

            def ln_spread(v, prev=True):
                pe.wait_ge(diag_ready, v + 1)
                if prev:
                    pe.wait_ge(ln_done, v)
                pe.matmul(PS[:, RB, :], ONES[:, :], DIAG, start=True, stop=True).then_inc(rb_ready, 1)

            def ln(v, rhs, ready, value):
                ln_center(v, rhs, ready, value)
                ln_var(v)
                ln_spread(v)

            def attn_start(inv, lay):
                pe.wait_ge(attn_w, pe.snap(lay * (16 * A_DMAS) + (inv * DEPTH + 1) * 16 * A_DMAS))

            def project(part, p, b):
                at = (2 * part + b) * 512
                return pe.matmul(PS[:, RAW + b, :], XS[:, p, :], WQKV[:, at:at + 512], start=True, stop=True)

            def turn(src, pairs):
                for n, (bank, pair) in enumerate(pairs):
                    at = (n % 4) * P
                    mm = pe.matmul(PS[:, bank, at:at + P], src(pair), EYE[:, :], is_transpose=True, start=True,
                                   stop=True, skip_group_check=True)
                return mm

            both = [(TQ + h // 4, h) for h in range(NP_)]

            def turn_qk(g):
                for qk in range(2):
                    mm = turn(lambda h: V[:, qk, 2 * h:2 * h + 2, :].rearrange("p r d -> p (r d)"),
                              [(TQ + qk, 4 * g + j) for j in range(4)])
                return mm

            def score(q, heads):
                for j in heads:
                    for w in range(NW):
                        for r in range(2):
                            mm = pe.matmul(PS[WIN * w:WIN * (w + 1), SB + r, j * 2 * WIN:(j + 1) * 2 * WIN],
                                           QT[DH * r:DH * (r + 1), q, j, WIN * w:WIN * (w + 1)],
                                           KT[DH * r:DH * (r + 1), q, j, WIN * w:WIN * (w + 2)],
                                           start=False, stop=True, skip_group_check=True)
                return mm

            def weigh(p, pairs):
                for j in pairs:
                    for w in range(NW):
                        for r in range(2):
                            mm = pe.matmul(PS[WIN * w:WIN * (w + 1), OB + r, j * DH:(j + 1) * DH],
                                           PT[DH * r:DH * (r + 1), j, WIN * w:WIN * (w + 1)],
                                           V2[DH * r:DH * (r + 1), p, w, j * DH:(j + 1) * DH],
                                           start=True, stop=True, skip_group_check=True)
                return mm

            def step(p, i, c, v2):
                a, b, cc, d = stages(i)
                q = 1 - p
                if a:
                    pe.wait_ge(xs_ready, c(1))
                    if past(i, 1):
                        pe.wait_ge(v0_evac, c(0))
                    project(0, p, 0)
                if d:
                    weigh(q, range(4, 6))
                if a:
                    if past(i, 1):
                        pe.wait_ge(v_evac, c(0))
                    project(0, p, 1).then_inc(raw_q, 1)
                if d:
                    weigh(q, range(6, 8)).then_inc(o_ready, 1)
                if cc:
                    score(p, range(4, 6))
                if a:
                    pe.wait_ge(sq_q, c(1))
                    project(1, p, 0)
                if d:
                    pe.wait_ge(on_ready, c(-2))
                    turn(lambda h: ON[:, 2 * h:2 * h + 2, :].rearrange("p r d -> p (r d)"), both).then_inc(to_ready, 1)
                if a:
                    project(1, p, 1).then_inc(raw_k, 1)
                if cc:
                    score(p, range(6, 8)).then_inc(s_ready, 1)
                if d:
                    pe.wait_ge(otev, c(-2))
                    for h in range(NP_):
                        mm = pe.matmul(PS[:, OB, 0:P], WO[:, h, :], OT[:, h, :], start=(h == 0), stop=(h == NP_ - 1))
                    mm.then_inc(wo_ready, 1)
                if b:
                    pe.wait_ge(rot_ready, c(0))
                    turn_qk(0).then_inc(t0_ready, 1)
                if a:
                    pe.wait_ge(sq_k, c(1))
                    project(2, p, 0).then_inc(raw_v0, 1)
                if b:
                    pe.wait_ge(tev0, c(0))
                    turn_qk(1).then_inc(t1_ready, 1)
                    pe.wait_ge(halo_ready, c(0))
                    if past(i, 2):
                        pe.wait_ge(sm_ready, c(-1))
                    for r in range(2):
                        pe.matmul(PS[:, SB + r, :], EYEB[:, :],
                                  rep(MASK[:, 1 if isinstance(i, int) and i == 1 else 0, :], [P, NP_, 2 * WIN], 1),
                                  start=True, stop=False, skip_group_check=True)
                    score(q, range(0, 2))
                if cc:
                    pe.wait_ge(e_ready, c(-1))
                    pe.wait_ge(v2_odd if p else v2_even, v2(-2))
                    if b:
                        pe.wait_ge(tev1, c(0))
                    turn(lambda j: PR[:, 2 * j:2 * j + 2, :].rearrange("p r k -> p (r k)"), both).then_inc(pt_ready, 1)
                if b:
                    score(q, range(2, 4))
                if cc:
                    pe.wait_ge(init, 5)
                    pe.wait_ge(ptev, c(-1))
                    if past(i, 3):
                        pe.wait_ge(xb_ready, c(-2))
                    weigh(p, range(0, 2))
                if a:
                    project(2, p, 1).then_inc(raw_v, 1)
                if cc:
                    weigh(p, range(2, 4))

            def ffn(inv, lay):
                L = pe.snap(lay * 4 + (lncount(inv) + 0))
                G = pe.snap(lay * 4 + inv * DEPTH * 4)
                G3 = pe.snap(lay * 12 + inv * DEPTH * 12)
                pe.wait_ge(ffn_w, pe.snap(lay * (16 * F_DMAS) + (inv * DEPTH + 1) * 16 * F_DMAS))

                def xf(g):
                    return pe.snap(G + g + 1)
                ln_center(pe.snap(L + 0), XF[:, :], xf_ready, xf(0))
                ln_var(pe.snap(L + 0))
                ln_spread(pe.snap(L + 0))
                for g in range(NG):
                    more = g + 1 < NG
                    v = pe.snap(L + (g + 1))
                    if more:
                        ln_center(v, XF[:, :], xf_ready, xf(g + 1))
                    pe.wait_ge(ln_done, v)
                    for t in range(6):
                        gate, n = t < 3, t % 3
                        if t == 3 and more:
                            ln_var(v)
                        if g == 0 and t < 4:
                            pass
                        elif t in (1, 2):
                            pe.wait_ge(ht_ready, pe.snap(G3 + (3 * g - 3 + t)))
                        elif t == 0:
                            pe.wait_ge(gelu_ready, pe.snap(G3 + 3 * g))
                        elif t == 3:
                            pe.wait_ge(ht_ready, pe.snap(G3 + 3 * g))
                        else:
                            pe.wait_ge(gelu_ready, pe.snap(G3 + (3 * g + t - 3)))
                        at, rows = FT[n]
                        at += DI if gate else 0
                        pe.matmul(PS[0:rows, HB + (6 * g + t) % 4, :], W1[:, at:at + rows], XN[:, g % 2, :],
                                  start=True, stop=True).then_inc(h_ready, 1)
                    if more:
                        ln_spread(v)
                    pe.wait_ge(ht_ready, pe.snap(G3 + (3 * g + 3)))
                    if g > 0:
                        pe.wait_ge(xa_ready, pe.snap(G + (g + 4 + 4 * inv)))
                    for n, (_, rows) in enumerate(FT):
                        mm = pe.matmul(PS[:, YB, :], W2[0:rows, n, :], HT[0:rows, n, :], start=(n == 0), stop=(n == 2))
                    mm.then_inc(y_ready, 1)

            stack = layers(pe, step, attn_start, ffn)

            def norm_in(inv):
                for g in range(NG):
                    v = 0 if inv == 0 else lncount(1) - 4
                    ready, value = (xr_ready, NG) if inv == 0 else (xr_mid, NG)
                    r = XR[:, g * GT:(g + 1) * GT]
                    ln_center(v + g, r, ready, value, prev=v + g > 0)
                    ln_var(v + g, prev=v + g > 0)
                    ln_spread(v + g, prev=v + g > 0)

            norm_in(0)
            stack(0)

            pe.wait_ge(mid_w, 16 * 6)
            v0 = 4 + 4 * DEPTH
            for g in range(NG):
                ln(v0 + 2 * g, XR[:, g * GT:(g + 1) * GT], xr_half, NG)
                ln(v0 + 2 * g + 1, XB[:, 1 + g * GT:1 + (g + 1) * GT], ln_done, v0 + 2 * g + 1)
                pe.wait_ge(ln_done, v0 + 2 * g + 2)
                if g > 0:
                    pe.wait_ge(mq_done, g)
                pe.matmul(PS[:, 3, :], WQM[:, :], XN[:, 0, :], start=True, stop=True).then_inc(mq_ready, 1)
                if g > 0:
                    pe.wait_ge(k4_ready, g)
                    pe.wait_ge(vx_ready, g)
                for j in range(4):
                    mm = pe.matmul(PS[:, 4 + j // 2, (j % 2) * 256:(j % 2 + 1) * 256], XN[:, 0, j * P:(j + 1) * P],
                                   WKVM[:, :], start=True, stop=True)
                mm.then_inc(mkv_ready, 1)
                pe.wait_ge(k4_ready, g + 1)
                pe.wait_ge(vx_ready, g + 1)
                for j in range(4):
                    mm = pe.matmul(PS[:, 7, 0:P + 1], K4[:, j, :], VX[:, j, :], start=(g == 0 and j == 0),
                                   stop=(g == NG - 1 and j == 3))
                mm.then_inc(kv_ready, 1)
            pe.wait_ge(kvm_ready, 1)
            for g in range(NG):
                q = QB[:, g * GT:(g + 1) * GT]
                if g == 0:
                    pe.wait_ge(mq_done, NG)
                else:
                    pe.wait_ge(mg_ready, g)
                pe.matmul(PS[:, 3, :], KVM, q, start=True, stop=True)
                pe.matmul(PS[:, 4, :], KSM, q, start=True, stop=True).then_inc(num_ready, 1)
                pe.wait_ge(ao_ready, g + 1)
                pe.matmul(PS[:, 5, :], PROJ[:, :], EL, start=True, stop=True).then_inc(proj_ready, 1)
                v = v0 + 2 * NG + g
                ln(v, XB[:, 1 + g * GT:1 + (g + 1) * GT], x1_ready, g + 1)
                pe.wait_ge(ln_done, v + 1)
                for n in range(4):
                    mm = pe.matmul(PS[:, 3 + n, :], FC1[:, n * P:(n + 1) * P], XN[:, 0, :], start=True, stop=True)
                mm.then_inc(mh_ready, 1)
                pe.wait_ge(mg_ready, g + 1)
                if g > 0:
                    pe.wait_ge(xr_mid, g)
                for n in range(4):
                    mm = pe.matmul(PS[:, 7, :], FC2[:, n, :], HT[:, n, :], start=(n == 0), stop=(n == 3))
                mm.then_inc(my_ready, 1)

            norm_in(1)
            stack(1)

            pe.wait_ge(xr_half, 2 * NG)
            for c in range(CH):
                mm = pe.transpose(PS[:, c // 4, (c % 4) * P:(c % 4 + 1) * P], XR[:, c * P:(c + 1) * P], EYE[:, :])
                if c % 4 == 3:
                    mm.then_inc(o_t, 1)

        @block.scalar
        def _(act):
            def ln(v, scale, prev=True):
                act.wait_ge(cen_ready, act.snap(v + 1) if not isinstance(v, int) else v + 1)
                act.activation(D2, PS[:, CEN, :], ACT.Square).then_inc(d2_ready, 1)
                if prev:
                    act.wait_ge(ln_done, v)
                act.activation(DG, PS[:, CEN, :], ACT.Copy, scale=scale).then_inc(dg_ready, 1)

            act.wait_ge(consts, 16 * 6)
            act.activation(MASK[:, :, :], MASKF[:, :, :], ACT.Copy)
            act.activation(EYEB[:, :], EYE[:, :], ACT.Copy).then_inc(cast, 1)
            for b in range(4):
                act.wait_ge(xt_ready, b + 1)
                act.activation(XR[:, b * GT:(b + 1) * GT], PS[:, b, :], ACT.Copy).then_inc(xr_ready, 1)

            def attn_start(inv, lay):
                act.wait_ge(init, 5)
                act.wait_ge(xa_ready, act.snap(lay * 4 + (inv * DEPTH * 4 + 4 + 4 * inv)))

            def step(p, i, c, v2):
                a, b, cc, d = stages(i)
                q = 1 - p
                src = PS[:, RAW:RAW + 2, :]

                def shift(at, buf):
                    act.activation(XS[0:DH, buf, :], XA[0:DH, bass.ds(at + 1, P)], ACT.Copy)
                    act.activation(XS[DH:P, buf, :], XA[DH:P, bass.ds(at, P)], ACT.Copy).then_inc(xs_ready, 1)

                def raw(k, ready, done):
                    act.wait_ge(ready, c(1))
                    act.activation(RAWQK[:, k].rearrange("p (b h) d -> p b (h d)", b=2), src, ACT.Copy)
                    act.activation(SQ[:, k].rearrange("p (b h) d -> p b (h d)", b=2), src, ACT.Square).then_inc(done, 1)

                def evac(g, ready, done):
                    act.wait_ge(ready, c(0))
                    act.activation(QT[:, q, 4 * g:4 * g + 4, :], PS[:, TQ, :].rearrange("p (j t) -> p j t", t=P), ACT.Copy)
                    act.activation(KT[:, q, 4 * g:4 * g + 4, WIN:], PS[:, TK, :].rearrange("p (j t) -> p j t", t=P),
                                   ACT.Copy).then_inc(done, 1)
                if isinstance(i, int) and i == 0:
                    shift(0, 0)
                if a:
                    if past(i, 1):
                        act.wait_ge(qn_ready, c(0))
                    raw(0, raw_q, sq_q)
                if d:
                    act.wait_ge(to_ready, c(-2))
                    act.activation(OT[:, :, :].rearrange("p (b j) t -> p b (j t)", b=2), PS[:, TQ:TQ + 2, :],
                                   ACT.Copy).then_inc(otev, 1)
                if a:
                    raw(1, raw_k, sq_k)
                if cc:
                    act.wait_ge(sm_ready, c(-1))
                    if past(i, 3):
                        act.wait_ge(pt_ready, c(-2))
                        act.wait_ge(rs_ready, c(-2))
                    act.activation(paired(PR[:, :, :]), split(SM[:, :, :]), ACT.Exp,
                                   scale=QK_SCALE).then_inc(e_ready, 1)
                if b:
                    evac(0, t0_ready, tev0)
                    evac(1, t1_ready, tev1)
                    if past(i, 2):
                        act.wait_ge(s_ready, c(-1))
                    act.wait_ge(tev1, c(0))
                    act.activation(KT[:, p, :, 0:WIN], KT[:, q, :, P:P + WIN], ACT.Copy,
                                   scale=NEXT[:, :]).then_inc(halo_ready, 1)
                if cc:
                    act.wait_ge(pt_ready, c(-1))
                    act.activation(PT[:, :, :].rearrange("p (b j) t -> p b (j t)", b=2), PS[:, TQ:TQ + 2, :],
                                   ACT.Copy).then_inc(ptev, 1)
                if a and not (isinstance(i, int) and i == CH - 1):
                    if past(i, 1):
                        act.wait_ge(raw_v, c(0))
                    shift(i * P + P, q)
                if a:
                    act.wait_ge(raw_v0, c(1))
                    if past(i, 2):
                        act.wait_ge(v2_odd if p else v2_even, v2(-2))
                    if past(i, 1):
                        act.wait_ge(v2_even if p else v2_odd, v2(-1))
                    act.activation(VS[:, p, 0:512], PS[:, RAW, :], ACT.Copy).then_inc(v0_evac, 1)
                    act.wait_ge(raw_v, c(1))
                    act.activation(VS[:, p, 512:], PS[:, RAW + 1, :], ACT.Copy).then_inc(v_evac, 1)

            def ffn(inv, lay):
                L = act.snap(lay * 4 + lncount(inv))
                G3 = act.snap(lay * 12 + inv * DEPTH * 12)
                H6 = act.snap(lay * 24 + inv * DEPTH * 24)
                act.wait_ge(ffn_w, act.snap(lay * (16 * F_DMAS) + (inv * DEPTH + 1) * 16 * F_DMAS))

                def shifted(g):
                    if g > 0:
                        act.wait_ge(cen_ready, act.snap(L + g))
                    at = g * GT
                    act.activation(XF[0:DH, :], XB[0:DH, at + 1:at + 1 + GT], ACT.Copy)
                    act.activation(XF[DH:P, :], XB[DH:P, at:at + GT], ACT.Copy).then_inc(xf_ready, 1)

                act.wait_ge(xb_ready, act.snap(lay * CH + (inv * DEPTH + 1) * CH))
                shifted(0)
                ln(L, SMALL[:, S_G:S_G + 1])
                for g in range(NG):
                    if g + 1 < NG:
                        shifted(g + 1)
                        ln(act.snap(L + (g + 1)), SMALL[:, S_G:S_G + 1])
                    for n, (_, rows) in enumerate(FT):
                        act.wait_ge(h_ready, act.snap(H6 + (6 * g + n + 1)))
                        if g > 0:
                            act.wait_ge(ht_ready, act.snap(G3 + (3 * g - 2 + n)))
                        act.activation(GB[0:rows, n, :], PS[0:rows, HB + (6 * g + n) % 4, :], ACT.Gelu,
                                       bias=SMALL[0:rows, S_B1G + n:S_B1G + n + 1]).then_inc(gelu_ready, 1)

            stack = layers(act, step, attn_start, ffn)
            for g in range(NG):
                ln(g, 1.0, prev=g > 0)
            stack(0)

            act.wait_ge(mid_w, 16 * 6)
            v0 = 4 + 4 * DEPTH
            for g in range(NG):
                ln(v0 + 2 * g, 1.0)
                ln(v0 + 2 * g + 1, MSMALL[:, M_G1:M_G1 + 1])
                act.wait_ge(el_q, g + 1)
                act.activation(EL, EL, ACT.Exp).then_inc(ex_q, 1)
                act.wait_ge(mkv_ready, g + 1)
                if g > 0:
                    act.wait_ge(kv_ready, g)
                act.activation(VX[:, :, 0:P], PS[:, 4:6, :].rearrange("p b (j t) -> p (b j) t", j=2)[:, :, P:2 * P],
                               ACT.Copy).then_inc(vx_ready, 1)
                act.wait_ge(el_k, g + 1)
                act.activation(EL, EL, ACT.Exp).then_inc(ex_k, 1)
            for g in range(NG):
                ln(v0 + 2 * NG + g, MSMALL[:, M_G2:M_G2 + 1])
                act.wait_ge(mh_ready, g + 1)
                if g > 0:
                    act.wait_ge(my_ready, g)
                for n in range(4):
                    ins = act.activation(HT[:, n, :], PS[:, 3 + n, :], ACT.Gelu,
                                         bias=MSMALL[:, M_FC1B + n:M_FC1B + n + 1])
                ins.then_inc(mg_ready, 1)
            for g in range(NG):
                ln(lncount(1) - 4 + g, 1.0)
            stack(1)
            for b in range(4):
                act.wait_ge(o_t, b + 1)
                act.activation(XIO[:, 4 * b:4 * b + 4, :], PS[:, b, :].rearrange("p (c d) -> p c d", d=P),
                               ACT.Copy).then_inc(o_c, 1)

        @block.vector
        def _(dve):
            dve.memset(ONES[:, :], 1.0).then_inc(init, 1)
            dve.memset(MEAN[:, :], 1.0 / P).then_inc(init, 1)
            dve.memset(XA[:, 0:1], 0.0).then_inc(init, 1)
            dve.memset(XB[:, 0:1], 0.0).then_inc(init, 1)
            dve.memset(VX[:, :, P:P + 1], 1.0).then_inc(init, 1)
            dve.memset(VS[:, 1, :], 0.0).then_inc(o_ready, 2)
            dve.memset(KT[:, 0, :, 0:WIN], 0.0).then_inc(halo_ready, 1)

            def rsqrt(y, x, half, u, eps, eps_op):
                dve.tensor_scalar(x, x, eps, None, eps_op)
                dve.drain()
                dve.tensor_scalar(half, x, -0.5, None, ALU.mult)
                dve.tensor_scalar(u.bitcast(I32), x.bitcast(I32), 1, None, ALU.logical_shift_right)
                dve.drain()
                dve.tensor_scalar(y.bitcast(I32), u.bitcast(I32), -1.0, RSQRT_MAGIC, ALU.mult, ALU.add)
                for n in range(3):
                    dve.drain()
                    dve.tensor_tensor(u, y, half, ALU.mult)
                    dve.drain()
                    dve.tensor_tensor(u, u, y, ALU.mult)
                    dve.drain()
                    last = dve.scalar_tensor_tensor(y, u, 1.5, y, ALU.add, ALU.mult)
                return last

            def value(v, k):
                return v + k if isinstance(v, int) else dve.snap(v + k)

            def ln_rstd(v):
                dve.wait_ge(var_ready, value(v, 1))
                dve.tensor_copy(V4[:, :], PS[:, VAR, 0:4])
                dve.drain()
                rsqrt(R4[:, :], V4[:, :], NX4[:, :], NU4[:, :], EPS, ALU.add).then_inc(r4_ready, 1)
                dve.drain()

            def ln_diag(v, prev=True):
                if prev:
                    dve.wait_ge(rb_ready, v)
                for j in range(4):
                    ins = dve.tensor_scalar(DIAG[:, j * P:(j + 1) * P], EYE[:, :], R4[:, j:j + 1], None, ALU.mult)
                ins.then_inc(diag_ready, 1)

            def ln_apply(v, o, bias=None, done=None):
                dve.wait_ge(rb_ready, value(v, 1))
                dve.wait_ge(dg_ready, value(v, 1))
                ins = dve.tensor_tensor(o, DG, PS[:, RB, :], ALU.mult)
                if bias is not None:
                    dve.drain()
                    ins = dve.tensor_scalar(o, o, bias, None, ALU.add)
                ins.then_inc(ln_done, 1)
                if done is not None:
                    dve.engine_nop().then_inc(done, 1)

            def attn_start(inv, lay):
                pass

            def step(p, i, c, v2):
                a, b, cc, d = stages(i)
                if d:
                    dve.wait_ge(o_ready, c(0))
                    rsum = SUM[:, :].rearrange("p (j r) -> p r j", r=2).unsqueeze(3).broadcast_to([P, 2, NP_, DH])
                    dve.tensor_tensor(split(ON[:, :, :]), PS[:, OB:OB + 2, :].rearrange("p r (j d) -> p r j d", d=DH),
                                      rsum, ALU.mult).then_inc(on_ready, 1)
                if a:
                    dve.wait_ge(sq_q, c(1))
                    dve.tensor_reduce(SS[:, 0:HEADS], SQ[:, 0], AX.X, ALU.add)
                if cc:
                    dve.wait_ge(s_ready, c(-1))
                    sc = PS[:, SB:SB + 2, :].rearrange("p b (j k) -> p (b j) k", k=2 * WIN)
                    dve.tensor_reduce(MX[:, :], sc, AX.X, ALU.max)
                    dve.drain()
                    dve.tensor_tensor(SM[:, :, :], sc, rep(MX[:, :], [P, HEADS, 2 * WIN], 2),
                                      ALU.subtract).then_inc(sm_ready, 1)
                if a:
                    dve.wait_ge(sq_k, c(1))
                    dve.tensor_reduce(SS[:, HEADS:2 * HEADS], SQ[:, 1], AX.X, ALU.add)
                if d:
                    dve.wait_ge(wo_ready, c(-2))
                    at = (i - 3) * P + 1
                    dve.tensor_tensor(XB[:, bass.ds(at, P)], PS[:, OB, 0:P], XA[:, bass.ds(at, P)],
                                      ALU.add).then_inc(xb_ready, 1)
                if a:
                    dve.drain()
                    rsqrt(RN[:, :, :].rearrange("p a b -> p (a b)"), SS[:, :], NX[:, :], NU[:, :], 1e-24, ALU.max)
                    dve.drain()
                    if past(i, 1):
                        dve.wait_ge(vv_ready, c(0))
                    for k in range(2):
                        ins = dve.tensor_tensor(QN[:, k], RAWQK[:, k], rep(RN[:, k, :], [P, HEADS, DH], 2), ALU.mult)
                    ins.then_inc(qn_ready, 1)
                if cc:
                    dve.wait_ge(e_ready, c(-1))
                    dve.tensor_reduce(SUM[:, :], PR[:, :, :], AX.X, ALU.add)
                if a or cc:
                    dve.drain()
                if cc:
                    dve.reciprocal(SUM[:, :], SUM[:, :]).then_inc(rs_ready, 1)
                if a:
                    dve.wait_ge(tab_ready, c(1))
                    if past(i, 1):
                        dve.wait_ge(rot_ready, c(0))
                    for k in range(2):
                        ins = dve.tensor_tensor(paired(U[:, k]), split(QN[:, k]),
                                                per_dim(TAB[:, 2 * k * DH:(2 * k + 1) * DH], DH), ALU.mult)
                    ins.then_inc(u_ready, 1)
                if cc:
                    dve.drain()

            def ffn(inv, lay):
                L = dve.snap(lay * 4 + lncount(inv))
                G = dve.snap(lay * 4 + inv * DEPTH * 4)
                G3 = dve.snap(lay * 12 + inv * DEPTH * 12)
                H6 = dve.snap(lay * 24 + inv * DEPTH * 24)
                dve.wait_ge(ffn_w, dve.snap(lay * (16 * F_DMAS) + (inv * DEPTH + 1) * 16 * F_DMAS))
                ln_rstd(L)
                ln_diag(L)
                ln_apply(L, XN[:, 0, :], SMALL[:, S_B:S_B + 1])
                for g in range(NG):
                    v = dve.snap(L + (g + 1))
                    if g + 1 < NG:
                        ln_rstd(v)
                        ln_diag(v)
                    for n, (_, rows) in enumerate(FT):
                        dve.wait_ge(h_ready, dve.snap(H6 + (6 * g + n + 4)))
                        dve.wait_ge(gelu_ready, dve.snap(G3 + (3 * g + n + 1)))
                        if g > 0:
                            dve.wait_ge(y_ready, dve.snap(G + g))
                        dve.scalar_tensor_tensor(HT[0:rows, n, :], PS[0:rows, HB + (6 * g + n + 3) % 4, :],
                                                 SMALL[0:rows, S_B1A + n:S_B1A + n + 1], GB[0:rows, n, :],
                                                 ALU.add, ALU.mult).then_inc(ht_ready, 1)
                    if g + 1 < NG:
                        ln_apply(v, XN[:, (g + 1) % 2, :], SMALL[:, S_B:S_B + 1])
                    dve.wait_ge(y_ready, dve.snap(G + (g + 1)))
                    s = slice(1 + g * GT, 1 + (g + 1) * GT)
                    dve.scalar_tensor_tensor(XA[:, s], PS[:, YB, :], SMALL[:, S_B2:S_B2 + 1], XB[:, s],
                                             ALU.add, ALU.add).then_inc(xa_ready, 1)

            stack = layers(dve, step, attn_start, ffn)

            def norm_in(v, inv):
                for g in range(NG):
                    ln_rstd(v + g)
                    ln_diag(v + g, prev=v + g > 0)
                    ln_apply(v + g, XA[:, 1 + g * GT:1 + (g + 1) * GT], done=xa_ready)

            def add_half():
                for g in range(NG):
                    r = XR[:, g * GT:(g + 1) * GT]
                    dve.scalar_tensor_tensor(r, XA[:, 1 + g * GT:1 + (g + 1) * GT], 0.5, r,
                                             ALU.mult, ALU.add).then_inc(xr_half, 1)

            norm_in(0, 0)
            stack(0)
            dve.drain()
            add_half()

            dve.wait_ge(consts, 16 * 6)
            dve.wait_ge(mid_w, 16 * 6)
            v0 = 4 + 4 * DEPTH
            for g in range(NG):
                s = slice(1 + g * GT, 1 + (g + 1) * GT)
                ln_rstd(v0 + 2 * g)
                ln_diag(v0 + 2 * g)
                ln_apply(v0 + 2 * g, XB[:, s])
                ln_rstd(v0 + 2 * g + 1)
                ln_diag(v0 + 2 * g + 1)
                ln_apply(v0 + 2 * g + 1, XN[:, 0, :], MSMALL[:, M_B1:M_B1 + 1])
                dve.wait_ge(mq_ready, g + 1)
                dve.tensor_scalar(EL, PS[:, 3, :], 0.0, None, ALU.min).then_inc(el_q, 1)
                dve.wait_ge(ex_q, g + 1)
                dve.scalar_tensor_tensor(QB[:, g * GT:(g + 1) * GT], PS[:, 3, :], 0.0, EL, ALU.max,
                                         ALU.add).then_inc(mq_done, 1)
                dve.drain()
                dve.wait_ge(mkv_ready, g + 1)
                keys = PS[:, 4:6, :].rearrange("p b (j t) -> p (b j) t", j=2)[:, :, 0:P]
                ek = EL.rearrange("p (j t) -> p j t", t=P)
                dve.wait_ge(vx_ready, g + 1)
                dve.tensor_scalar(ek, keys, 0.0, None, ALU.min).then_inc(el_k, 1)
                dve.wait_ge(ex_k, g + 1)
                if g > 0:
                    dve.wait_ge(kv_ready, g)
                dve.scalar_tensor_tensor(K4, keys, 0.0, ek, ALU.max, ALU.add).then_inc(k4_ready, 1)
                dve.drain()
            dve.wait_ge(kv_ready, NG)
            dve.tensor_copy(KS1[:, :], PS[:, 7, P:P + 1])
            dve.tensor_tensor(KVM, PS[:, 7, 0:P], BLOCKS[:, :], ALU.mult)
            dve.drain()
            dve.tensor_scalar(KSM, BLOCKS[:, :], KS1[:, :], None, ALU.mult).then_inc(kvm_ready, 1)
            for g in range(NG):
                s = slice(1 + g * GT, 1 + (g + 1) * GT)
                den = XF[:, :]
                dve.wait_ge(num_ready, g + 1)
                dve.tensor_scalar(den, PS[:, 4, :], 1e-6, None, ALU.add)
                dve.drain()
                dve.reciprocal(den, den)
                dve.drain()
                dve.tensor_tensor(EL, PS[:, 3, :], den, ALU.mult).then_inc(ao_ready, 1)
                dve.wait_ge(proj_ready, g + 1)
                dve.scalar_tensor_tensor(XB[:, s], PS[:, 5, :], MSMALL[:, M_PB:M_PB + 1], XB[:, s], ALU.add,
                                         ALU.add).then_inc(x1_ready, 1)
                v = v0 + 2 * NG + g
                ln_rstd(v)
                ln_diag(v)
                ln_apply(v, XN[:, 0, :], MSMALL[:, M_B2:M_B2 + 1])
                dve.wait_ge(my_ready, g + 1)
                dve.scalar_tensor_tensor(XB[:, s], PS[:, 7, :], MSMALL[:, M_FC2B:M_FC2B + 1], XB[:, s], ALU.add, ALU.add)
                dve.drain()
                r = XR[:, g * GT:(g + 1) * GT]
                dve.tensor_tensor(r, r, XB[:, s], ALU.add).then_inc(xr_mid, 1)
            norm_in(lncount(1) - 4, 1)
            stack(1)
            dve.drain()
            add_half()

        @block.gpsimd
        def _(pool):
            pool.wait_ge(consts, 16 * 6)

            def attn_start(inv, lay):
                pool.wait_ge(attn_w, pool.snap(lay * (16 * A_DMAS) + (inv * DEPTH + 1) * 16 * A_DMAS))

            def step(p, i, c, v2):
                if not stages(i)[0]:
                    return
                if past(i, 1):
                    pool.wait_ge(rot_ready, c(0))
                rot = ROT[:, bass.ds(i, 1), :].rearrange("p a b -> p (a b)")
                pool.tensor_tensor(TAB[:, :], rot, QKS[:, :], ALU.mult).then_inc(tab_ready, 1)
                pool.wait_ge(tab_ready, c(1))
                pool.wait_ge(qn_ready, c(1))
                if past(i, 1):
                    pool.wait_ge(t1_ready, c(0))
                half = DH // 2
                for k in range(2):
                    for h in range(2):
                        t = TAB[:, (2 * k + 1) * DH + h * half:(2 * k + 1) * DH + (h + 1) * half]
                        ins = pool.tensor_tensor(paired(V[:, k])[:, :, :, h * half:(h + 1) * half],
                                                 split(QN[:, k])[:, :, :, (1 - h) * half:(2 - h) * half],
                                                 per_dim(t, half), ALU.mult)
                ins.then_inc(vv_ready, 1)
                pool.wait_ge(u_ready, c(1))
                pool.wait_ge(vv_ready, c(1))
                for k in range(2):
                    ins = pool.tensor_tensor(V[:, k], V[:, k], U[:, k], ALU.add)
                ins.then_inc(rot_ready, 1)

            def ffn(inv, lay):
                pass

            stack = layers(pool, step, attn_start, ffn)
            stack(0)
            stack(1)

        @block.sync
        def _(sp):
            for t, n in ((EYE, "c_eye"), (CENTER, "c_center"), (BLOCKS, "c_blocks"), (NEXT, "c_next")):
                sp.dma_start(t[:, :], a[n]).then_inc(consts, 16)
            sp.dma_start(MASKF[:, :, :].rearrange("p a b -> p (a b)"), a["c_masks"]).then_inc(consts, 16)
            sp.dma_start(XIO, a["x"].rearrange("b (c p) d -> p (b c) d", p=P)).then_inc(x_in, 16)
            sp.dma_start(ROT[:, :, :].rearrange("p a b -> p (a b)"), a["c_rot"]).then_inc(consts, 16)

            def load_attn(lay):
                sp.dma_start(WQKV[:, :], a["wqkv"][bass.ds(lay, 1)].rearrange("l p n -> p (l n)")).then_inc(attn_w, 16)
                sp.dma_start(WO[:, :, :], a["wo"][bass.ds(lay, 1)].rearrange("l (h p) n -> p (l h) n", p=P)).then_inc(attn_w, 16)
                sp.dma_start(QKS[:, :], a["qks"][bass.ds(lay, 1), :].broadcast_to([P, 4 * DH])).then_inc(attn_w, 16)

            def load_ffn(lay):
                sp.dma_start(W1[:, :], a["w1"][bass.ds(lay, 1)].rearrange("l p n -> p (l n)")).then_inc(ffn_w, 16)
                sp.dma_start(W2[0:FT[0][1], 0:2, :],
                             a["w2"][bass.ds(lay, 1), 0:FT[2][0]].rearrange("l (i p) n -> p (l i) n", i=2)).then_inc(ffn_w, 16)
                sp.dma_start(W2[0:FT[2][1], 2, :],
                             a["w2"][bass.ds(lay, 1), FT[2][0]:DI].rearrange("l p n -> p (l n)")).then_inc(ffn_w, 16)
                sp.dma_start(SMALL[:, :], a["small"][bass.ds(lay, 1)].rearrange("l p n -> p (l n)")).then_inc(ffn_w, 16)

            load_attn(0)
            for t, n in ((WQM, "m_q"), (WKVM, "m_kv"), (PROJ, "m_proj"), (FC1, "m_fc1"), (MSMALL, "m_small")):
                sp.dma_start(t[:, :], a[n]).then_inc(mid_w, 16)
            sp.dma_start(FC2[:, :, :], a["m_fc2"].rearrange("(n p) d -> p n d", p=P)).then_inc(mid_w, 16)

            def attn_start(inv, lay):
                sp.wait_ge(init, 5)
                if inv == 0:
                    sp.wait_ge(xa_ready, sp.snap(lay * 4 + 4))
                else:
                    sp.wait_ge(xa_ready, sp.snap(lay * 4 + (DEPTH * 4 + 8)))
                load_ffn(lay)

            def step(p, i, c, v2):
                if not stages(i)[0]:
                    return
                done = v2_odd if p else v2_even
                sp.wait_ge(v_evac, c(1))
                sp.wait_ge(o_ready, c(1))
                for r in range(2):
                    cols = slice(r * 512, (r + 1) * 512)
                    for w in range(NW):
                        own = VS[WIN * w:WIN * (w + 1), p, cols]
                        before = VS[WIN * (w - 1):WIN * w, p, cols] if w else VS[P - WIN:P, 1 - p, cols]
                        sp.dma_start(V2[DH * r:DH * r + WIN, p, w, :], before).then_inc(done, 16)
                        sp.dma_start(V2[DH * r + WIN:DH * (r + 1), p, w, :], own).then_inc(done, 16)

            def ffn(inv, lay):
                sp.wait_ge(init, 5)
                sp.wait_ge(xb_ready, sp.snap(lay * CH + (inv * DEPTH + 1) * CH))
                load_attn(lay + 1)

            sp.wait_ge(init, 5)
            sp.wait_ge(halo_ready, 1)
            stack = layers(sp, step, attn_start, ffn)
            stack(0)
            stack(1)
            sp.wait_ge(attn_w, 16 * A_DMAS * (2 * DEPTH + 1))
            for b in range(4):
                sp.wait_ge(o_c, b + 1)
                sp.dma_start(out.rearrange("b (c p) d -> p (b c) d", p=P)[:, 4 * b:4 * b + 4, :],
                             XIO[:, 4 * b:4 * b + 4, :]).then_inc(stored, 16)
            sp.wait_ge(stored, 16 * 4)


def kernel(**inputs):
    import concourse.bacc as bacc
    from concourse.bass_utils import run_bass_kernel_spmd

    def get(name):
        return np.ascontiguousarray(inputs[name])

    def again(w):
        return np.concatenate([w, w[:1]], 0)

    def swapped(w):
        return np.concatenate([w[:, DH // 2:], w[:, :DH // 2]], 1)

    def tiles(v):
        cols = np.zeros((v.shape[0], P, 3), v.dtype)
        for n, (at, rows) in enumerate(FT):
            cols[:, :rows, n] = v[:, at:at + rows]
        return cols

    b1 = get("L0_ffn_b1")
    qs, ks = get("L0_ffn_q_scale"), get("L0_ffn_k_scale")
    small = np.concatenate([get("L0_ffn_ln_g")[:, :, None], get("L0_ffn_ln_b")[:, :, None],
                            get("L0_ffn_b2")[:, :, None], tiles(b1[:, :DI]), tiles(b1[:, DI:])], 2)
    mid = np.concatenate([get(n).reshape(P, 1) for n in (
        "L0_attn_norm1_g", "L0_attn_norm1_b", "L0_attn_proj_b", "L0_attn_norm2_g", "L0_attn_norm2_b",
        "L0_attn_fc2_b")] + [get("L0_attn_fc1_b").reshape(4, P).T], 1)
    arrays = {
        "x": get("L0_attn_x"),
        "wqkv": again(get("L0_ffn_Wqkv")), "wo": again(get("L0_ffn_Wo")),
        "qks": again(np.concatenate([qs, swapped(qs), ks, swapped(ks)], 1)),
        "w1": get("L0_ffn_W1"), "w2": get("L0_ffn_W2"), "small": small,
        "m_q": get("L0_attn_qkv_w")[:P].T, "m_kv": get("L0_attn_qkv_w")[P:].T,
        "m_proj": get("L0_attn_proj_w").T, "m_fc1": get("L0_attn_fc1_w").T, "m_fc2": get("L0_attn_fc2_w").T,
        "m_small": mid, **shape_constants(),
    }
    arrays = {n: np.ascontiguousarray(v) for n, v in arrays.items()}
    nc = bacc.Bacc("TRN2", target_bir_lowering=False, num_devices=1)
    aps = {n: nc.dram_tensor(n, v.shape, mybir.dt.from_np(v.dtype), kind="ExternalInput").ap() for n, v in arrays.items()}
    out = nc.dram_tensor("out", (1, NTOK, P), F32, kind="ExternalOutput").ap()
    build(nc, aps, out)
    got = run_bass_kernel_spmd(nc, [arrays], core_ids=[0])
    return got.results[0]["out"]
```

```python
from contextlib import ExitStack

import numpy as np

import concourse.bass as bass
from concourse import mybir

F32 = mybir.dt.float32
BF16 = mybir.dt.bfloat16
I32 = mybir.dt.int32
ALU = mybir.AluOpType
ACT = mybir.ActivationFunctionType
AX = mybir.AxisListType

P = 128
NTOK = 2048
CH = 16
GT = 512
NG = NTOK // GT
DEPTH = 6
HEADS = 16
DH = 64
NP_ = HEADS // 2
WIN = 32
NW = P // WIN
DI = 341
FT = [(0, 114), (114, 114), (228, 113)]
MH = 8
EPS = 1e-5
QK_SCALE = 8.0
MASKED = -1.0e30
RSQRT_MAGIC = float(0x5F3759DF)

RAW, TQ, TK, SB, OB = 0, 2, 3, 4, 6
CEN, VAR, RB, YB = 0, 1, 1, 7
HB = (4, 5, 2, 3)

S_G, S_B, S_B2, S_B1A, S_B1G, NSMALL = 0, 1, 2, 3, 6, 9
M_G1, M_B1, M_PB, M_G2, M_B2, M_FC2B, M_FC1B, NMSMALL = 0, 1, 2, 3, 4, 5, 6, 10


def shape_constants():
    half = np.arange(0, DH, 2, dtype=np.float32)
    inv_freq = (1.0 / np.float32(10000.0) ** (half / np.float32(DH))).astype(np.float32)
    tok = np.arange(NTOK, dtype=np.float32)
    freqs = (tok[:, None] * inv_freq[None, :]).astype(np.float32).astype(np.float64)
    base = ((half + np.float32(0.4 * DH)) / np.float32(1.4 * DH)).astype(np.float32).astype(np.float64)
    power = (np.arange(NTOK) % P) / (WIN // 2)
    scale = base[None, :] ** power[:, None]
    cos, sin = np.cos(freqs), np.sin(freqs)
    rot = np.concatenate(
        [np.concatenate([cos, cos, -sin, sin], 1) * np.tile(s, 4) for s in (scale, 1.0 / scale)], 1)
    rot = rot.astype(np.float32).reshape(CH, P, 4 * DH).transpose(1, 0, 2)
    to_next = np.tile(base ** (P / (WIN // 2)), 4).astype(np.float32).reshape(P, 1)
    q, k = np.arange(P)[:, None] % WIN, np.arange(2 * WIN)[None, :]
    seen = (k - WIN <= q) & (q <= k)
    first = seen & ((k >= WIN) | (np.arange(P)[:, None] >= WIN))
    masks = np.stack([np.where(m, 0.0, MASKED) for m in (seen, first)], 1).astype(np.float32)
    blocks = (np.arange(P)[:, None] // MH == np.arange(P)[None, :] // MH).astype(np.float32)
    eye = np.eye(P, dtype=np.float32)
    return {
        "c_rot": np.ascontiguousarray(rot.reshape(P, CH * 4 * DH)),
        "c_next": to_next,
        "c_masks": np.ascontiguousarray(masks.reshape(P, 4 * WIN)),
        "c_blocks": blocks,
        "c_eye": eye,
        "c_center": (eye - np.float32(1.0 / P)).astype(np.float32),
    }


def build(nc, a, out):
    ctx = ExitStack()
    with ctx:
        def sb(name, shape, dt=F32):
            return ctx.enter_context(nc.sbuf_tensor(name, shape, dt))

        def sem(name):
            return ctx.enter_context(nc.semaphore(name))

        XR = sb("XR", [P, NTOK])
        XA = sb("XA", [P, NTOK + 1])
        XB = sb("XB", [P, NTOK + 1])
        ROT = sb("ROT", [P, CH, 4 * DH])
        NEXT = sb("NEXT", [P, 1])
        MASKF = sb("MASKF", [P, 2, 2 * WIN])
        MASK = sb("MASK", [P, 2, 2 * WIN], BF16)
        EYE = sb("EYE", [P, P])
        EYEB = sb("EYEB", [P, P], BF16)
        CENTER = sb("CENTER", [P, P])
        BLOCKS = sb("BLOCKS", [P, P])
        ONES = sb("ONES", [P, P])
        MEAN = sb("MEAN", [P, 1])
        WQKV = sb("WQKV", [P, 3 * HEADS * DH])
        WO = sb("WO", [P, NP_, P])
        QKS = sb("QKS", [P, 4 * DH])
        W1 = sb("W1", [P, 2 * DI])
        W2 = sb("W2", [P, 3, P])
        SMALL = sb("SMALL", [P, NSMALL])
        XS = sb("XS", [P, 2, P])
        RAWQK = sb("RAWQK", [P, 2, HEADS, DH])
        SQ = sb("SQ", [P, 2, HEADS, DH])
        SS = sb("SS", [P, 2 * HEADS])
        NX = sb("NX", [P, 2 * HEADS])
        NU = sb("NU", [P, 2 * HEADS])
        RN = sb("RN", [P, 2, HEADS])
        TAB = sb("TAB", [P, 4 * DH])
        QN = sb("QN", [P, 2, HEADS, DH])
        U = sb("U", [P, 2, HEADS, DH])
        V = sb("V", [P, 2, HEADS, DH])
        QT = sb("QT", [P, 2, NP_, P])
        KT = sb("KT", [P, 2, NP_, WIN + P])
        MX = sb("MX", [P, HEADS])
        SM = sb("SM", [P, HEADS, 2 * WIN])
        SUM = sb("SUM", [P, HEADS])
        PR = sb("PR", [P, HEADS, 2 * WIN])
        PT = sb("PT", [P, NP_, P])
        VS = sb("VS", [P, 2, HEADS * DH])
        V2 = sb("V2", [P, 2, NW, NP_ * DH])
        ON = sb("ON", [P, HEADS, DH])
        OT = sb("OT", [P, NP_, P])
        XF = sb("XF", [P, GT])
        D2 = RAWQK[:, 0, 0:8, :].rearrange("p a b -> p (a b)")
        DG = RAWQK[:, 0, 8:16, :].rearrange("p a b -> p (a b)")
        DIAG = RAWQK[:, 1, 0:8, :].rearrange("p a b -> p (a b)")
        V4 = sb("V4", [P, 4])
        NX4 = sb("NX4", [P, 4])
        NU4 = sb("NU4", [P, 4])
        R4 = sb("R4", [P, 4])
        XN = sb("XN", [P, NG, GT])
        gb_ = QT[:, :, :, :].rearrange("p a b c -> p (a b c)")
        ht_ = KT[:, :, :, :].rearrange("p a b c -> p (a b c)")
        GB = gb_[:, 0:3 * GT].rearrange("p (i t) -> p i t", t=GT)
        HT = ht_[:, 0:4 * GT].rearrange("p (i t) -> p i t", t=GT)
        DG4 = U[:, :, :, :].rearrange("p a b c -> p (a b c)").rearrange("p (g t) -> p g t", t=GT)
        v_flat = V[:, :, :, :].rearrange("p a b c -> p (a b c)")
        D2M = v_flat[:, 0:2 * GT].rearrange("p (g t) -> p g t", t=GT)
        DIAGM = v_flat[:, 2 * GT:4 * GT].rearrange("p (g t) -> p g t", t=GT)
        HTM = (HT, DG4)
        XIO = QN[:, :, :, :].rearrange("p a b c -> p (a b c)").rearrange("p (c d) -> p c d", d=P)
        WQ_M = QKS[:, 0:P]
        WQM = sb("WQM", [P, P])
        WKVM = sb("WKVM", [P, 2 * P])
        PROJ = sb("PROJ", [P, P])
        FC1 = sb("FC1", [P, 4 * P])
        FC2 = sb("FC2", [P, 4, P])
        MSMALL = sb("MSMALL", [P, NMSMALL])
        QB = QT[:, :, :, :].rearrange("p a b c -> p (a b c)")
        EL = SQ[:, :, :, :].rearrange("p a b c -> p (a b c)").rearrange("p (g t) -> p g t", t=GT)
        K4 = SM[:, :, :].rearrange("p a b -> p (a b)")[:, 0:GT].rearrange("p (j d) -> p j d", d=P)
        VX = sb("VX", [P, 4, P + 1])
        KVM = PR[:, 0:2, :].rearrange("p a b -> p (a b)")
        KSM = PR[:, 2:4, :].rearrange("p a b -> p (a b)")
        KS1 = sb("KS1", [P, 1])

        PS = ctx.enter_context(nc.psum_tensor("PS", [P, 8, 512], F32))

        consts = sem("consts"); init = sem("init"); cast = sem("cast")
        attn_w = sem("attn_w"); ffn_w = sem("ffn_w"); mid_w = sem("mid_w")
        xs_ready = sem("xs_ready"); tab_ready = sem("tab_ready")
        raw_q = sem("raw_q"); raw_k = sem("raw_k"); raw_v = sem("raw_v")
        sq_q = sem("sq_q"); sq_k = sem("sq_k"); v_evac = sem("v_evac")
        cp_q = sem("cp_q"); cp_k = sem("cp_k"); ptev0 = sem("ptev0"); raw_v0 = sem("raw_v0"); v0_evac = sem("v0_evac")
        qn_ready = sem("qn_ready"); u_ready = sem("u_ready"); vv_ready = sem("vv_ready"); rot_ready = sem("rot_ready")
        t0_ready = sem("t0_ready"); t1_ready = sem("t1_ready")
        tev0 = sem("tev0"); tev1 = sem("tev1"); halo_ready = sem("halo_ready")
        s_ready = sem("s_ready"); sm_ready = sem("sm_ready"); e_ready = sem("e_ready")
        rs_ready = sem("rs_ready"); on_ready = sem("on_ready"); to_ready = sem("to_ready")
        pt_ready = sem("pt_ready"); ptev = sem("ptev")
        v2_even = sem("v2_even"); v2_odd = sem("v2_odd")
        o_ready = sem("o_ready"); otev = sem("otev"); wo_ready = sem("wo_ready"); xb_ready = sem("xb_ready")
        xa_ready = sem("xa_ready")
        xf_ready = sem("xf_ready"); cen_ready = sem("cen_ready"); d2_ready = sem("d2_ready")
        dg_ready = sem("dg_ready"); var_ready = sem("var_ready"); r4_ready = sem("r4_ready")
        diag_ready = sem("diag_ready"); rb_ready = sem("rb_ready"); ln_done = sem("ln_done")
        h_ready = sem("h_ready"); gelu_ready = sem("gelu_ready"); ht_ready = sem("ht_ready"); y_ready = sem("y_ready")
        m_cen = sem("m_cen"); m_d2 = sem("m_d2"); m_dg = sem("m_dg"); m_var = sem("m_var"); m_r = sem("m_r")
        m_diag = sem("m_diag"); m_rb = sem("m_rb"); m_ln = sem("m_ln")
        x_in = sem("x_in"); xt_ready = sem("xt_ready"); xr_ready = sem("xr_ready")
        mq_ready = sem("mq_ready"); mkv_ready = sem("mkv_ready"); el_q = sem("el_q"); el_k = sem("el_k")
        ex_q = sem("ex_q"); ex_k = sem("ex_k"); mq_done = sem("mq_done"); k4_ready = sem("k4_ready")
        vx_ready = sem("vx_ready"); kv_ready = sem("kv_ready"); kvm_ready = sem("kvm_ready")
        num_ready = sem("num_ready"); ao_ready = sem("ao_ready"); proj_ready = sem("proj_ready")
        x1_ready = sem("x1_ready"); mh_ready = sem("mh_ready"); mg_ready = sem("mg_ready")
        my_ready = sem("my_ready"); xr_mid = sem("xr_mid"); xr_half = sem("xr_half")
        o_t = sem("o_t"); o_c = sem("o_c"); stored = sem("stored")

        def val(eng, x):
            return x if isinstance(x, int) else eng.snap(x)

        def lncount(inv):
            return 1 + 4 * DEPTH * inv

        A_DMAS, F_DMAS, V2_DMAS = 3, 4, 16
        V2_INC = 16 * V2_DMAS

        def split(ap):
            return ap.rearrange("p (r j) d -> p r j d", r=2)

        def paired(ap):
            return ap.rearrange("p (j r) d -> p r j d", r=2)

        def per_dim(ap, n):
            return ap.unsqueeze(1).unsqueeze(1).broadcast_to([P, 2, NP_, n])

        def rep(ap, shape, axis):
            return ap.unsqueeze(axis).broadcast_to(shape)

        def stages(i):
            if not isinstance(i, int):
                return True, True, True, True
            return i < CH, 1 <= i <= CH, 2 <= i <= CH + 1, 3 <= i <= CH + 2

        def past(i, n):
            return not isinstance(i, int) or i >= n

        block = ctx.enter_context(nc.Block())

        def layers(eng, attn_step, attn_start, ffn, norm_before=None, norm_within=None, parts=3):
            ahead = norm_before is not None

            def counter(start):
                kept = {}

                def count(k):
                    if k not in kept:
                        kept[k] = val(eng, start + k)
                    return kept[k]
                return count

            def stack(inv):
                def layer(lay, last):
                    first = val(eng, lay * CH + inv * DEPTH * CH)

                    def v2_at(pairs):
                        return val(eng, lay * (CH // 2 * V2_INC) + (inv * DEPTH * CH // 2 + pairs) * V2_INC)

                    if not ahead:
                        attn_start(inv, lay)
                    for i in range(1 if ahead else 0, 4):
                        attn_step(i % 2, i, counter(first + i), lambda off, i=i: v2_at((i + off) // 2 + 1))
                    with eng.Fori(0, CH // 2 - 3) as j:
                        at = val(eng, first + j * 2)
                        c = counter(at + 4)
                        v2j = val(eng, lay * (CH // 2 * V2_INC) + j * V2_INC + (inv * DEPTH * CH // 2) * V2_INC)
                        for p in (0, 1):
                            attn_step(p, val(eng, j * 2 + (4 + p)), lambda k, p=p: c(k + p),
                                      lambda off, p=p: val(eng, v2j + ((4 + p + off) // 2 + 1) * V2_INC))
                    c = counter(first + CH)
                    for i in range(CH - 2, CH + 3):
                        within = None
                        if i >= CH and ahead:
                            norm_before(inv, lay, i - CH)
                            within = lambda i=i: norm_within(inv, lay, i - CH)
                        attn_step(i % 2, i, lambda k, i=i: c(k + i - CH), lambda off, i=i: v2_at((i + off) // 2 + 1),
                                  within)

                    def start_next(part):
                        if not last:
                            if part == 0:
                                attn_start(inv, val(eng, lay + 1))
                            attn_step(0, 0, c, None, part=part)
                    ffn(inv, lay, start_next)
                if not ahead:
                    with eng.Fori(0, DEPTH) as lay:
                        layer(lay, False)
                else:
                    attn_start(inv, 0)
                    for part in range(parts):
                        attn_step(0, 0, counter(inv * DEPTH * CH), None, part=part)
                    with eng.Fori(0, DEPTH - 1) as lay:
                        layer(lay, False)
                    layer(DEPTH - 1, True)
            return stack

        @block.tensor
        def _(pe):
            pe.wait_ge(consts, 16 * 6)
            pe.wait_ge(init, 5)
            pe.wait_ge(cast, 1)
            pe.wait_ge(x_in, 16)
            for c in range(CH):
                mm = pe.transpose(PS[:, c // 4, (c % 4) * P:(c % 4 + 1) * P], XIO[:, c, :], EYE[:, :])
                if c % 4 == 3:
                    mm.then_inc(xt_ready, 1)

            def ln_center(v, rhs, ready, value):
                pe.wait_ge(ready, value)
                pe.wait_ge(dg_ready, v)
                pe.matmul(PS[:, CEN, :], CENTER[:, :], rhs, start=True, stop=True).then_inc(cen_ready, 1)

            def ln_var(v):
                pe.wait_ge(d2_ready, v + 1)
                pe.wait_ge(ln_done, v)
                for j in range(4):
                    mm = pe.matmul(PS[:, VAR, j:j + 1], D2[:, j * P:(j + 1) * P], MEAN[:, :], start=True, stop=True)
                mm.then_inc(var_ready, 1)

            def ln_spread(v):
                pe.wait_ge(diag_ready, v + 1)
                pe.matmul(PS[:, RB, :], ONES[:, :], DIAG, start=True, stop=True).then_inc(rb_ready, 1)

            def norm_all(b, rhs, ready, values):
                def variance(g):
                    n = 4 * b + g
                    pe.wait_ge(m_d2, n + 1)
                    if g == 0 and b > 0:
                        pe.wait_ge(m_r, b)
                    for j in range(4):
                        mm = pe.matmul(PS[:, VAR, 4 * g + j:4 * g + j + 1], D2M[:, n % 2, j * P:(j + 1) * P],
                                       MEAN[:, :], start=True, stop=True)
                    mm.then_inc(m_var, 1)
                for g in range(NG):
                    n = 4 * b + g
                    pe.wait_ge(ready, values[g])
                    if n >= 2:
                        pe.wait_ge(m_dg, n - 1)
                    pe.matmul(PS[:, 2 * (n % 2), :], CENTER[:, :], rhs(g), start=True, stop=True).then_inc(m_cen, 1)
                    if g > 0:
                        variance(g - 1)
                variance(NG - 1)
                for g in range(NG):
                    n = 4 * b + g
                    pe.wait_ge(m_diag, n + 1)
                    if n >= 2:
                        pe.wait_ge(m_ln, n - 1)
                    pe.matmul(PS[:, 5 + n % 2, :], ONES[:, :], DIAGM[:, n % 2, :], start=True, stop=True).then_inc(m_rb, 1)

            def attn_start(inv, lay):
                pe.wait_ge(attn_w, val(pe, lay * (16 * A_DMAS) + (inv * DEPTH + 1) * 16 * A_DMAS))

            def project(part, p, b):
                at = (2 * part + b) * 512
                return pe.matmul(PS[:, RAW + b, :], XS[:, p, :], WQKV[:, at:at + 512], start=True, stop=True)

            def turn(src, pairs):
                for n, (bank, pair) in enumerate(pairs):
                    at = (n % 4) * P
                    mm = pe.matmul(PS[:, bank, at:at + P], src(pair), EYE[:, :], is_transpose=True, start=True,
                                   stop=True, skip_group_check=True)
                return mm

            both = [(TQ + h // 4, h) for h in range(NP_)]

            def turn_qk(g):
                for qk in range(2):
                    mm = turn(lambda h: V[:, qk, 2 * h:2 * h + 2, :].rearrange("p r d -> p (r d)"),
                              [(TQ + qk, 4 * g + j) for j in range(4)])
                return mm

            def score(q, heads):
                for j in heads:
                    for w in range(NW):
                        for r in range(2):
                            mm = pe.matmul(PS[WIN * w:WIN * (w + 1), SB + r, j * 2 * WIN:(j + 1) * 2 * WIN],
                                           QT[DH * r:DH * (r + 1), q, j, WIN * w:WIN * (w + 1)],
                                           KT[DH * r:DH * (r + 1), q, j, WIN * w:WIN * (w + 2)],
                                           start=False, stop=True, skip_group_check=True)
                return mm

            def weigh(p, pairs):
                for j in pairs:
                    for w in range(NW):
                        for r in range(2):
                            mm = pe.matmul(PS[WIN * w:WIN * (w + 1), OB + r, j * DH:(j + 1) * DH],
                                           PT[DH * r:DH * (r + 1), j, WIN * w:WIN * (w + 1)],
                                           V2[DH * r:DH * (r + 1), p, w, j * DH:(j + 1) * DH],
                                           start=True, stop=True, skip_group_check=True)
                return mm

            def step(p, i, c, v2, within=None, part=None):
                if part is not None:
                    pe.wait_ge((xs_ready, cp_q, cp_k)[part], c(1))
                    mm = project(part, p, 0)
                    if part == 2:
                        mm.then_inc(raw_v0, 1)
                    project(part, p, 1).then_inc((raw_q, raw_k, raw_v)[part], 1)
                    return
                a, b, cc, d = stages(i)
                q = 1 - p
                if a:
                    pe.wait_ge(xs_ready, c(1))
                    if past(i, 1):
                        pe.wait_ge(v0_evac, c(0))
                    if d:
                        pe.wait_ge(ptev, c(-2))
                    project(0, p, 0)
                if d:
                    weigh(q, range(4, 6))
                if a:
                    if past(i, 1):
                        pe.wait_ge(v_evac, c(0))
                    project(0, p, 1).then_inc(raw_q, 1)
                if d:
                    weigh(q, range(6, 8)).then_inc(o_ready, 1)
                if within and not cc:
                    within()
                if cc:
                    score(p, range(4, 6))
                if a:
                    pe.wait_ge(cp_q, c(1))
                    project(1, p, 0)
                if d:
                    pe.wait_ge(on_ready, c(-2))
                    turn(lambda h: ON[:, 2 * h:2 * h + 2, :].rearrange("p r d -> p (r d)"), both).then_inc(to_ready, 1)
                if a:
                    project(1, p, 1).then_inc(raw_k, 1)
                if cc:
                    score(p, range(6, 8)).then_inc(s_ready, 1)
                if d:
                    pe.wait_ge(otev, c(-2))
                    for h in range(NP_):
                        mm = pe.matmul(PS[:, OB, 0:P], WO[:, h, :], OT[:, h, :], start=(h == 0), stop=(h == NP_ - 1))
                    mm.then_inc(wo_ready, 1)
                if within and cc:
                    within()
                if b:
                    pe.wait_ge(rot_ready, c(0))
                    turn_qk(0).then_inc(t0_ready, 1)
                if a:
                    pe.wait_ge(cp_k, c(1))
                    project(2, p, 0).then_inc(raw_v0, 1)
                if b:
                    pe.wait_ge(tev0, c(0))
                    turn_qk(1).then_inc(t1_ready, 1)
                    pe.wait_ge(halo_ready, c(0))
                    if past(i, 2):
                        pe.wait_ge(sm_ready, c(-1))
                    for r in range(2):
                        pe.matmul(PS[:, SB + r, :], EYEB[:, :],
                                  rep(MASK[:, 1 if isinstance(i, int) and i == 1 else 0, :], [P, NP_, 2 * WIN], 1),
                                  start=True, stop=False, skip_group_check=True)
                    score(q, range(0, 2))
                if cc:
                    pe.wait_ge(e_ready, c(-1))
                    pe.wait_ge(v2_odd if p else v2_even, v2(-2))
                    if b:
                        pe.wait_ge(tev1, c(0))
                    turn(lambda j: PR[:, 2 * j:2 * j + 2, :].rearrange("p r k -> p (r k)"), both).then_inc(pt_ready, 1)
                if b:
                    score(q, range(2, 4))
                if cc:
                    pe.wait_ge(init, 5)
                    pe.wait_ge(ptev0, c(-1))
                    if past(i, 3):
                        pe.wait_ge(xb_ready, c(-2))
                    weigh(p, range(0, 2))
                if a:
                    project(2, p, 1).then_inc(raw_v, 1)
                if cc:
                    weigh(p, range(2, 4))

            def norm_before(inv, lay, g):
                L = val(pe, lay * 4 + lncount(inv))
                if g == 0:
                    pe.wait_ge(v_evac, val(pe, lay * CH + (inv * DEPTH + 1) * CH))
                else:
                    ln_spread(val(pe, L + (g - 1)))
                if g < 3:
                    pe.wait_ge(ptev, val(pe, lay * CH + (inv * DEPTH * CH + CH + g - 2)))
                ln_center(val(pe, L + g), XF[:, :], xf_ready, val(pe, lay * 4 + (inv * DEPTH * 4 + g + 1)))

            def hidden(inv, lay, g, tiles):
                G3 = lay * 12 + inv * DEPTH * 12
                for t in tiles:
                    gate, n = t < 3, t % 3
                    if g == 0 and t < 4:
                        if t == 2:
                            pe.wait_ge(xb_ready, val(pe, lay * CH + (inv * DEPTH + 1) * CH))
                    elif t in (1, 2):
                        pe.wait_ge(ht_ready, val(pe, G3 + (3 * g - 3 + t)))
                    elif t == 0:
                        pe.wait_ge(gelu_ready, val(pe, G3 + 3 * g))
                    elif t == 3:
                        pe.wait_ge(ht_ready, val(pe, G3 + 3 * g))
                    else:
                        pe.wait_ge(gelu_ready, val(pe, G3 + (3 * g + t - 3)))
                    at, rows = FT[n]
                    at += DI if gate else 0
                    pe.matmul(PS[0:rows, HB[(6 * g + t) % 4], :], W1[:, at:at + rows], XN[:, g, :],
                              start=True, stop=True).then_inc(h_ready, 1)

            def norm_within(inv, lay, g):
                ln_var(val(pe, lay * 4 + (lncount(inv) + g)))
                if g == 2:
                    pe.wait_ge(ffn_w, val(pe, lay * (16 * F_DMAS) + (inv * DEPTH + 1) * 16 * F_DMAS))
                    pe.wait_ge(sm_ready, val(pe, lay * CH + (inv * DEPTH + 1) * CH))
                    pe.wait_ge(ln_done, val(pe, lay * 4 + (lncount(inv) + 1)))
                    hidden(inv, lay, 0, range(0, 2))

            def ffn(inv, lay, start_next):
                L = val(pe, lay * 4 + (lncount(inv) + 0))
                G = val(pe, lay * 4 + inv * DEPTH * 4)
                G3 = val(pe, lay * 12 + inv * DEPTH * 12)
                hidden(inv, lay, 0, range(2, 3))
                norm_before(inv, lay, NG - 1)
                hidden(inv, lay, 0, range(3, 6))
                ln_var(val(pe, L + (NG - 1)))
                for g in range(NG):
                    if g + 1 < NG:
                        pe.wait_ge(ln_done, val(pe, L + (g + 2)))
                        hidden(inv, lay, g + 1, range(0, 3))
                    if g > 0:
                        if g == 1:
                            pe.wait_ge(ln_done, val(pe, L + NG))
                        start_next(g - 1)
                    pe.wait_ge(ht_ready, val(pe, G3 + (3 * g + 3)))
                    if g > 0:
                        pe.wait_ge(xa_ready, val(pe, G + (g + 4 + 4 * inv)))
                    for n, (_, rows) in enumerate(FT):
                        mm = pe.matmul(PS[:, YB, :], W2[0:rows, n, :], HT[0:rows, n, :], start=(n == 0), stop=(n == 2))
                    mm.then_inc(y_ready, 1)
                    if g + 1 < NG:
                        hidden(inv, lay, g + 1, range(3, 6))
                    if g == 0:
                        ln_spread(val(pe, L + (NG - 1)))

            stack = layers(pe, step, attn_start, ffn, norm_before, norm_within)

            def group(x, g, at=0):
                return x[:, at + g * GT:at + (g + 1) * GT]

            norm_all(0, lambda g: group(XR, g), xr_ready, [NG] * NG)
            stack(0)

            pe.wait_ge(mid_w, 16 * 6)
            norm_all(1, lambda g: group(XR, g), xr_half, [1, 2, 3, 4])
            norm_all(2, lambda g: group(XB, g, 1), m_ln, [5, 6, 7, 8])

            def sum_kv(g):
                pe.wait_ge(k4_ready, g + 1)
                pe.wait_ge(vx_ready, g + 1)
                for j in range(4):
                    mm = pe.matmul(PS[:, 7, 0:P + 1], K4[:, j, :], VX[:, j, :], start=(g == 0 and j == 0),
                                   stop=(g == NG - 1 and j == 3))
                mm.then_inc(kv_ready, 1)
            pe.wait_ge(m_dg, 12)
            for g in range(NG):
                pe.wait_ge(m_ln, 9 + g)
                if g >= 2:
                    pe.wait_ge(mq_done, g - 1)
                pe.matmul(PS[:, 2 * (g % 2), :], WQM[:, :], XN[:, g, :], start=True, stop=True).then_inc(mq_ready, 1)
                if g > 0:
                    sum_kv(g - 1)
                for j in range(4):
                    mm = pe.matmul(PS[:, 3 + j // 2, (j % 2) * 256:(j % 2 + 1) * 256], XN[:, g, j * P:(j + 1) * P],
                                   WKVM[:, :], start=True, stop=True)
                mm.then_inc(mkv_ready, 1)
            sum_kv(NG - 1)
            pe.wait_ge(kvm_ready, 1)
            pe.wait_ge(mq_done, NG)

            def project_out(g):
                pe.wait_ge(ao_ready, g + 1)
                if g >= 2:
                    pe.wait_ge(x1_ready, g - 1)
                pe.matmul(PS[:, 2 * (g % 2), :], PROJ[:, :], EL[:, g % 2, :], start=True, stop=True).then_inc(proj_ready, 1)
            for g in range(NG):
                q = group(QB, g)
                if g >= 2:
                    pe.wait_ge(ao_ready, g - 1)
                pe.matmul(PS[:, 3 + 2 * (g % 2), :], KVM, q, start=True, stop=True)
                pe.matmul(PS[:, 4 + 2 * (g % 2), :], KSM, q, start=True, stop=True).then_inc(num_ready, 1)
                if g > 0:
                    project_out(g - 1)
            project_out(NG - 1)
            norm_all(3, lambda g: group(XB, g, 1), x1_ready, [NG] * NG)

            def fc2(g):
                pe.wait_ge(mg_ready, 4 * g + 4)
                if g > 0:
                    pe.wait_ge(xr_mid, g)
                for n in range(4):
                    mm = pe.matmul(PS[:, 7, :], FC2[:, n, :], HTM[g % 2][:, n, :], start=(n == 0), stop=(n == 3))
                mm.then_inc(my_ready, 1)
            pe.wait_ge(m_ln, 16)
            for g in range(NG):
                for n in range(4):
                    if g > 0:
                        pe.wait_ge(mg_ready, 4 * g - 3 + n)
                    pe.matmul(PS[:, 3 + n, :], FC1[:, n * P:(n + 1) * P], XN[:, g, :], start=True,
                              stop=True).then_inc(mh_ready, 1)
                if g > 0:
                    fc2(g - 1)
            fc2(NG - 1)

            norm_all(4, lambda g: group(XR, g), xr_mid, [NG] * NG)
            stack(1)

            pe.wait_ge(xr_half, 2 * NG)
            for c in range(CH):
                mm = pe.transpose(PS[:, c // 4, (c % 4) * P:(c % 4 + 1) * P], XR[:, c * P:(c + 1) * P], EYE[:, :])
                if c % 4 == 3:
                    mm.then_inc(o_t, 1)

        @block.scalar
        def _(act):
            def ln(v, scale):
                act.wait_ge(cen_ready, val(act, v + 1))
                act.activation(D2, PS[:, CEN, :], ACT.Square).then_inc(d2_ready, 1)
                act.wait_ge(ln_done, v)
                act.activation(DG, PS[:, CEN, :], ACT.Copy, scale=scale).then_inc(dg_ready, 1)

            act.wait_ge(consts, 16 * 6)
            act.activation(MASK[:, :, :], MASKF[:, :, :], ACT.Copy)
            act.activation(EYEB[:, :], EYE[:, :], ACT.Copy).then_inc(cast, 1)
            for b in range(4):
                act.wait_ge(xt_ready, b + 1)
                act.activation(XR[:, b * GT:(b + 1) * GT], PS[:, b, :], ACT.Copy).then_inc(xr_ready, 1)

            def attn_start(inv, lay):
                act.wait_ge(init, 5)
                act.wait_ge(xa_ready, val(act, lay * 4 + (inv * DEPTH * 4 + 1 + 4 * inv)))
                act.wait_ge(ln_done, val(act, lay * 4 + lncount(inv)))

            def step(p, i, c, v2, within=None, part=None):
                a, b, cc, d = stages(i)
                q = 1 - p
                src = PS[:, RAW:RAW + 2, :]

                def shift(at, buf):
                    act.activation(XS[0:DH, buf, :], XA[0:DH, bass.ds(at + 1, P)], ACT.Copy)
                    act.activation(XS[DH:P, buf, :], XA[DH:P, bass.ds(at, P)], ACT.Copy).then_inc(xs_ready, 1)

                def raw(k, ready, copied, done):
                    act.wait_ge(ready, c(1))
                    act.activation(RAWQK[:, k].rearrange("p (b h) d -> p b (h d)", b=2), src, ACT.Copy).then_inc(copied, 1)
                    act.wait_ge(copied, c(1))
                    act.activation(SQ[:, k], RAWQK[:, k], ACT.Square).then_inc(done, 1)

                def evac(g, ready, done):
                    act.wait_ge(ready, c(0))
                    act.activation(QT[:, q, 4 * g:4 * g + 4, :], PS[:, TQ, :].rearrange("p (j t) -> p j t", t=P), ACT.Copy)
                    act.activation(KT[:, q, 4 * g:4 * g + 4, WIN:], PS[:, TK, :].rearrange("p (j t) -> p j t", t=P),
                                   ACT.Copy).then_inc(done, 1)
                def keep_values(half):
                    act.wait_ge((raw_v0, raw_v)[half], c(1))
                    act.activation(VS[:, p, half * 512:(half + 1) * 512], PS[:, RAW + half, :],
                                   ACT.Copy).then_inc((v0_evac, v_evac)[half], 1)

                if part is not None:
                    if part == 0:
                        shift(0, 0)
                    elif part == 1:
                        raw(0, raw_q, cp_q, sq_q)
                    elif part == 2:
                        raw(1, raw_k, cp_k, sq_k)
                        shift(P, 1)
                    else:
                        keep_values(0)
                        keep_values(1)
                    return
                if a:
                    if past(i, 1):
                        act.wait_ge(qn_ready, c(0))
                    raw(0, raw_q, cp_q, sq_q)
                if d:
                    act.wait_ge(to_ready, c(-2))
                    act.activation(OT[:, :, :].rearrange("p (b j) t -> p b (j t)", b=2), PS[:, TQ:TQ + 2, :],
                                   ACT.Copy).then_inc(otev, 1)
                if a:
                    raw(1, raw_k, cp_k, sq_k)
                if b:
                    evac(0, t0_ready, tev0)
                if cc:
                    act.wait_ge(sm_ready, c(-1))
                    if past(i, 3):
                        act.wait_ge(pt_ready, c(-2))
                        act.wait_ge(rs_ready, c(-2))
                    act.activation(paired(PR[:, :, :]), split(SM[:, :, :]), ACT.Exp,
                                   scale=QK_SCALE).then_inc(e_ready, 1)
                if b:
                    evac(1, t1_ready, tev1)
                    if past(i, 2):
                        act.wait_ge(s_ready, c(-1))
                    act.wait_ge(tev1, c(0))
                    act.activation(KT[:, p, :, 0:WIN], KT[:, q, :, P:P + WIN], ACT.Copy,
                                   scale=NEXT[:, :]).then_inc(halo_ready, 1)
                if cc:
                    act.wait_ge(pt_ready, c(-1))
                    act.activation(PT[:, 0:4, :].rearrange("p j t -> p (j t)"), PS[:, TQ, :], ACT.Copy).then_inc(ptev0, 1)
                    act.activation(PT[:, 4:8, :].rearrange("p j t -> p (j t)"), PS[:, TK, :], ACT.Copy).then_inc(ptev, 1)
                if a and not (isinstance(i, int) and i == CH - 1):
                    if past(i, 1):
                        act.wait_ge(raw_v, c(0))
                    shift(i * P + P, q)
                if a:
                    if past(i, 2):
                        act.wait_ge(v2_odd if p else v2_even, v2(-2))
                    if past(i, 1):
                        act.wait_ge(v2_even if p else v2_odd, v2(-1))
                    keep_values(0)
                    keep_values(1)

            def norm_before(inv, lay, g):
                L = val(act, lay * 4 + lncount(inv))
                if g == 0:
                    act.wait_ge(ffn_w, val(act, lay * (16 * F_DMAS) + (inv * DEPTH + 1) * 16 * F_DMAS))
                    act.wait_ge(qn_ready, val(act, lay * CH + (inv * DEPTH + 1) * CH))
                else:
                    act.wait_ge(cen_ready, val(act, L + g))
                act.wait_ge(xb_ready, val(act, lay * CH + (inv * DEPTH * CH + 4 * g + 4)))
                at = g * GT
                act.activation(XF[0:DH, :], XB[0:DH, at + 1:at + 1 + GT], ACT.Copy)
                act.activation(XF[DH:P, :], XB[DH:P, at:at + GT], ACT.Copy).then_inc(xf_ready, 1)
                ln(val(act, L + g), SMALL[:, S_G:S_G + 1])

            def norm_within(inv, lay, g):
                pass

            def ffn(inv, lay, start_next):
                G3 = val(act, lay * 12 + inv * DEPTH * 12)
                H6 = val(act, lay * 24 + inv * DEPTH * 24)
                norm_before(inv, lay, NG - 1)
                for g in range(NG):
                    if g == 2:
                        start_next(0)
                    for n, (_, rows) in enumerate(FT):
                        act.wait_ge(h_ready, val(act, H6 + (6 * g + n + 1)))
                        if g > 0:
                            act.wait_ge(ht_ready, val(act, G3 + (3 * g - 2 + n)))
                        act.activation(GB[0:rows, n, :], PS[0:rows, HB[(6 * g + n) % 4], :], ACT.Gelu,
                                       bias=SMALL[0:rows, S_B1G + n:S_B1G + n + 1]).then_inc(gelu_ready, 1)
                    if g > 1:
                        start_next(g - 1)
                start_next(3)

            stack = layers(act, step, attn_start, ffn, norm_before, norm_within, parts=4)
            def norm_all(b, scale):
                for g in range(NG):
                    n = 4 * b + g
                    act.wait_ge(m_cen, n + 1)
                    if n >= 2:
                        act.wait_ge(m_var, n - 1)
                    act.activation(D2M[:, n % 2, :], PS[:, 2 * (n % 2), :], ACT.Square).then_inc(m_d2, 1)
                    if b > 0:
                        act.wait_ge(m_ln, n - 3)
                    act.activation(DG4[:, g, :], PS[:, 2 * (n % 2), :], ACT.Copy, scale=scale).then_inc(m_dg, 1)

            norm_all(0, 1.0)
            stack(0)

            act.wait_ge(mid_w, 16 * 6)
            norm_all(1, 1.0)
            norm_all(2, MSMALL[:, M_G1:M_G1 + 1])
            for g in range(NG):
                a = 2 * (g % 2)
                act.wait_ge(el_q, g + 1)
                act.activation(EL[:, a, :], EL[:, a, :], ACT.Exp).then_inc(ex_q, 1)
                act.wait_ge(mkv_ready, g + 1)
                if g > 0:
                    act.wait_ge(kv_ready, g)
                act.activation(VX[:, :, 0:P], PS[:, 3:5, :].rearrange("p b (j t) -> p (b j) t", j=2)[:, :, P:2 * P],
                               ACT.Copy).then_inc(vx_ready, 1)
                act.wait_ge(el_k, g + 1)
                act.activation(EL[:, a + 1, :], EL[:, a + 1, :], ACT.Exp).then_inc(ex_k, 1)
            norm_all(3, MSMALL[:, M_G2:M_G2 + 1])
            for g in range(NG):
                for n in range(4):
                    act.wait_ge(mh_ready, 4 * g + n + 1)
                    if g >= 2:
                        act.wait_ge(my_ready, g - 1)
                    act.activation(HTM[g % 2][:, n, :], PS[:, 3 + n, :], ACT.Gelu,
                                   bias=MSMALL[:, M_FC1B + n:M_FC1B + n + 1]).then_inc(mg_ready, 1)
            norm_all(4, 1.0)
            stack(1)
            for b in range(4):
                act.wait_ge(o_t, b + 1)
                act.activation(XIO[:, 4 * b:4 * b + 4, :], PS[:, b, :].rearrange("p (c d) -> p c d", d=P),
                               ACT.Copy).then_inc(o_c, 1)

        @block.vector
        def _(dve):
            dve.memset(ONES[:, :], 1.0).then_inc(init, 1)
            dve.memset(MEAN[:, :], 1.0 / P).then_inc(init, 1)
            dve.memset(XA[:, 0:1], 0.0).then_inc(init, 1)
            dve.memset(XB[:, 0:1], 0.0).then_inc(init, 1)
            dve.memset(VX[:, :, P:P + 1], 1.0).then_inc(init, 1)
            dve.memset(VS[:, 1, :], 0.0).then_inc(o_ready, 2)
            dve.memset(KT[:, 0, :, 0:WIN], 0.0).then_inc(halo_ready, 1)
            for first in (cen_ready, d2_ready, dg_ready, var_ready, r4_ready, diag_ready, rb_ready, ln_done):
                dve.engine_nop().then_inc(first, 1)

            def rsqrt(y, x, half, u, eps, eps_op):
                dve.tensor_scalar(x, x, eps, None, eps_op)
                dve.drain()
                dve.tensor_scalar(half, x, -0.5, None, ALU.mult)
                dve.tensor_scalar(u.bitcast(I32), x.bitcast(I32), 1, None, ALU.logical_shift_right)
                dve.drain()
                dve.tensor_scalar(y.bitcast(I32), u.bitcast(I32), -1.0, RSQRT_MAGIC, ALU.mult, ALU.add)
                for n in range(3):
                    dve.drain()
                    dve.tensor_tensor(u, y, half, ALU.mult)
                    dve.drain()
                    dve.tensor_tensor(u, u, y, ALU.mult)
                    dve.drain()
                    last = dve.scalar_tensor_tensor(y, u, 1.5, y, ALU.add, ALU.mult)
                return last

            def value(v, k):
                return val(dve, v + k)

            def ln_rstd(v):
                dve.wait_ge(var_ready, value(v, 1))
                dve.tensor_copy(V4[:, :], PS[:, VAR, 0:4])
                dve.drain()
                rsqrt(R4[:, :], V4[:, :], NX4[:, :], NU4[:, :], EPS, ALU.add).then_inc(r4_ready, 1)
                dve.drain()

            def ln_diag(v):
                dve.wait_ge(rb_ready, v)
                for j in range(4):
                    ins = dve.tensor_scalar(DIAG[:, j * P:(j + 1) * P], EYE[:, :], R4[:, j:j + 1], None, ALU.mult)
                ins.then_inc(diag_ready, 1)

            def ln_apply(v, o, bias):
                dve.wait_ge(rb_ready, value(v, 1))
                dve.wait_ge(dg_ready, value(v, 1))
                dve.tensor_tensor(o, DG, PS[:, RB, :], ALU.mult)
                dve.drain()
                dve.tensor_scalar(o, o, bias, None, ALU.add).then_inc(ln_done, 1)

            def attn_start(inv, lay):
                pass

            def normalise(i, c):
                dve.drain()
                rsqrt(RN[:, :, :].rearrange("p a b -> p (a b)"), SS[:, :], NX[:, :], NU[:, :], 1e-24, ALU.max)
                dve.drain()
                if past(i, 1):
                    dve.wait_ge(vv_ready, c(0))
                for k in range(2):
                    ins = dve.tensor_tensor(QN[:, k], RAWQK[:, k], rep(RN[:, k, :], [P, HEADS, DH], 2), ALU.mult)
                ins.then_inc(qn_ready, 1)

            def rotate(i, c):
                dve.wait_ge(tab_ready, c(1))
                if past(i, 1):
                    dve.wait_ge(rot_ready, c(0))
                for k in range(2):
                    ins = dve.tensor_tensor(paired(U[:, k]), split(QN[:, k]),
                                            per_dim(TAB[:, 2 * k * DH:(2 * k + 1) * DH], DH), ALU.mult)
                ins.then_inc(u_ready, 1)

            def step(p, i, c, v2, within=None, part=None):
                a, b, cc, d = stages(i)

                def sum_squares(k):
                    dve.wait_ge((sq_q, sq_k)[k], c(1))
                    dve.tensor_reduce(SS[:, k * HEADS:(k + 1) * HEADS], SQ[:, k], AX.X, ALU.add)
                if part is not None:
                    if part == 0:
                        sum_squares(0)
                    elif part == 1:
                        sum_squares(1)
                        normalise(i, c)
                    else:
                        dve.drain()
                        rotate(i, c)
                    return
                if d:
                    dve.wait_ge(o_ready, c(0))
                    rsum = SUM[:, :].rearrange("p (j r) -> p r j", r=2).unsqueeze(3).broadcast_to([P, 2, NP_, DH])
                    dve.tensor_tensor(split(ON[:, :, :]), PS[:, OB:OB + 2, :].rearrange("p r (j d) -> p r j d", d=DH),
                                      rsum, ALU.mult).then_inc(on_ready, 1)
                if within and not cc:
                    within()
                if a:
                    sum_squares(0)
                if cc:
                    dve.wait_ge(s_ready, c(-1))
                    sc = PS[:, SB:SB + 2, :].rearrange("p b (j k) -> p (b j) k", k=2 * WIN)
                    dve.tensor_reduce(MX[:, :], sc, AX.X, ALU.max)
                    dve.drain()
                    dve.tensor_tensor(SM[:, :, :], sc, rep(MX[:, :], [P, HEADS, 2 * WIN], 2),
                                      ALU.subtract).then_inc(sm_ready, 1)
                if a:
                    sum_squares(1)
                if d:
                    dve.wait_ge(wo_ready, c(-2))
                    at = (i - 3) * P + 1
                    dve.tensor_tensor(XB[:, bass.ds(at, P)], PS[:, OB, 0:P], XA[:, bass.ds(at, P)],
                                      ALU.add).then_inc(xb_ready, 1)
                if within and cc:
                    within()
                if a:
                    normalise(i, c)
                if cc:
                    dve.wait_ge(e_ready, c(-1))
                    dve.tensor_reduce(SUM[:, :], PR[:, :, :], AX.X, ALU.add)
                if a or cc:
                    dve.drain()
                if cc:
                    dve.reciprocal(SUM[:, :], SUM[:, :]).then_inc(rs_ready, 1)
                if a:
                    rotate(i, c)
                if cc:
                    dve.drain()

            def norm_before(inv, lay, g):
                if g == 0:
                    dve.wait_ge(ffn_w, val(dve, lay * (16 * F_DMAS) + (inv * DEPTH + 1) * 16 * F_DMAS))
                else:
                    ln_apply(val(dve, lay * 4 + (lncount(inv) + g - 1)), XN[:, g - 1, :], SMALL[:, S_B:S_B + 1])

            def norm_within(inv, lay, g):
                v = val(dve, lay * 4 + (lncount(inv) + g))
                ln_rstd(v)
                ln_diag(v)

            def ffn(inv, lay, start_next):
                G = val(dve, lay * 4 + inv * DEPTH * 4)
                G3 = val(dve, lay * 12 + inv * DEPTH * 12)
                H6 = val(dve, lay * 24 + inv * DEPTH * 24)
                norm_before(inv, lay, NG - 1)
                for g in range(NG):
                    for n, (_, rows) in enumerate(FT):
                        dve.wait_ge(h_ready, val(dve, H6 + (6 * g + n + 4)))
                        dve.wait_ge(gelu_ready, val(dve, G3 + (3 * g + n + 1)))
                        if g > 0:
                            dve.wait_ge(y_ready, val(dve, G + g))
                        dve.scalar_tensor_tensor(HT[0:rows, n, :], PS[0:rows, HB[(6 * g + n + 3) % 4], :],
                                                 SMALL[0:rows, S_B1A + n:S_B1A + n + 1], GB[0:rows, n, :],
                                                 ALU.add, ALU.mult).then_inc(ht_ready, 1)
                    if g == 0:
                        norm_within(inv, lay, NG - 1)
                    if g == 2:
                        start_next(0)
                    if g == 3:
                        start_next(1)
                    dve.wait_ge(y_ready, val(dve, G + (g + 1)))
                    s = slice(1 + g * GT, 1 + (g + 1) * GT)
                    dve.scalar_tensor_tensor(XA[:, s], PS[:, YB, :], SMALL[:, S_B2:S_B2 + 1], XB[:, s],
                                             ALU.add, ALU.add).then_inc(xa_ready, 1)
                    if g == 0:
                        norm_before(inv, lay, NG)
                start_next(2)

            stack = layers(dve, step, attn_start, ffn, norm_before, norm_within)

            def norm_all(b, o, bias=None, done=None):
                dve.wait_ge(m_var, 4 * b + 4)
                dve.tensor_copy(SS[:, 0:16], PS[:, VAR, 0:16])
                dve.drain()
                r = RN[:, 0, :]
                rsqrt(r, SS[:, 0:16], NX[:, 0:16], NU[:, 0:16], EPS, ALU.add).then_inc(m_r, 1)
                dve.drain()

                def apply(g):
                    n = 4 * b + g
                    dve.wait_ge(m_rb, n + 1)
                    dve.wait_ge(m_dg, n + 1)
                    ins = dve.tensor_tensor(o(g), DG4[:, g, :], PS[:, 5 + n % 2, :], ALU.mult)
                    if bias is not None:
                        dve.drain()
                        ins = dve.tensor_scalar(o(g), o(g), bias, None, ALU.add)
                    ins.then_inc(m_ln, 1)
                    if done is not None:
                        dve.engine_nop().then_inc(done, 1)
                for g in range(NG):
                    n = 4 * b + g
                    if n >= 2:
                        dve.wait_ge(m_rb, n - 1)
                    for j in range(4):
                        ins = dve.tensor_scalar(DIAGM[:, n % 2, j * P:(j + 1) * P], EYE[:, :],
                                                r[:, 4 * g + j:4 * g + j + 1], None, ALU.mult)
                    ins.then_inc(m_diag, 1)
                    if g > 0:
                        apply(g - 1)
                apply(NG - 1)

            def group(x, g, at=0):
                return x[:, at + g * GT:at + (g + 1) * GT]

            def add_half():
                for g in range(NG):
                    r = XR[:, g * GT:(g + 1) * GT]
                    dve.scalar_tensor_tensor(r, XA[:, 1 + g * GT:1 + (g + 1) * GT], 0.5, r,
                                             ALU.mult, ALU.add).then_inc(xr_half, 1)

            dve.wait_ge(consts, 16 * 6)
            norm_all(0, lambda g: group(XA, g, 1), done=xa_ready)
            stack(0)
            dve.drain()
            add_half()

            dve.wait_ge(mid_w, 16 * 6)
            norm_all(1, lambda g: group(XB, g, 1))
            norm_all(2, lambda g: XN[:, g, :], MSMALL[:, M_B1:M_B1 + 1])
            keys = PS[:, 3:5, :].rearrange("p b (j t) -> p (b j) t", j=2)[:, :, 0:P]
            for g in range(NG):
                a = 2 * (g % 2)
                eq, ek = EL[:, a, :], EL[:, a + 1, :].rearrange("p (j t) -> p j t", t=P)
                dve.wait_ge(mq_ready, g + 1)
                dve.tensor_scalar(eq, PS[:, a, :], 0.0, None, ALU.min).then_inc(el_q, 1)
                dve.wait_ge(mkv_ready, g + 1)
                dve.wait_ge(vx_ready, g + 1)
                dve.tensor_scalar(ek, keys, 0.0, None, ALU.min).then_inc(el_k, 1)
                dve.wait_ge(ex_q, g + 1)
                dve.scalar_tensor_tensor(group(QB, g), PS[:, a, :], 0.0, eq, ALU.max, ALU.add).then_inc(mq_done, 1)
                dve.wait_ge(ex_k, g + 1)
                if g > 0:
                    dve.wait_ge(kv_ready, g)
                dve.scalar_tensor_tensor(K4, keys, 0.0, ek, ALU.max, ALU.add).then_inc(k4_ready, 1)
            dve.drain()
            dve.wait_ge(kv_ready, NG)
            dve.tensor_copy(KS1[:, :], PS[:, 7, P:P + 1])
            dve.tensor_tensor(KVM, PS[:, 7, 0:P], BLOCKS[:, :], ALU.mult)
            dve.drain()
            dve.tensor_scalar(KSM, BLOCKS[:, :], KS1[:, :], None, ALU.mult).then_inc(kvm_ready, 1)

            def add_projected(g):
                dve.wait_ge(proj_ready, g + 1)
                dve.scalar_tensor_tensor(group(XB, g, 1), PS[:, 2 * (g % 2), :], MSMALL[:, M_PB:M_PB + 1],
                                         group(XB, g, 1), ALU.add, ALU.add).then_inc(x1_ready, 1)
            for g in range(NG):
                den = XF[:, :]
                dve.wait_ge(num_ready, g + 1)
                dve.tensor_scalar(den, PS[:, 4 + 2 * (g % 2), :], 1e-6, None, ALU.add)
                dve.drain()
                dve.reciprocal(den, den)
                dve.drain()
                dve.tensor_tensor(EL[:, g % 2, :], PS[:, 3 + 2 * (g % 2), :], den, ALU.mult).then_inc(ao_ready, 1)
                dve.drain()
                if g > 0:
                    add_projected(g - 1)
            add_projected(NG - 1)
            norm_all(3, lambda g: XN[:, g, :], MSMALL[:, M_B2:M_B2 + 1])
            for g in range(NG):
                x = group(XB, g, 1)
                dve.wait_ge(my_ready, g + 1)
                dve.scalar_tensor_tensor(x, PS[:, 7, :], MSMALL[:, M_FC2B:M_FC2B + 1], x, ALU.add, ALU.add)
                dve.drain()
                dve.tensor_tensor(group(XR, g), group(XR, g), x, ALU.add).then_inc(xr_mid, 1)
            norm_all(4, lambda g: group(XA, g, 1), done=xa_ready)
            stack(1)
            dve.drain()
            add_half()

        @block.gpsimd
        def _(pool):
            pool.wait_ge(consts, 16 * 6)

            def attn_start(inv, lay):
                pool.wait_ge(attn_w, pool.snap(lay * (16 * A_DMAS) + (inv * DEPTH + 1) * 16 * A_DMAS))

            def step(p, i, c, v2, within=None, part=None):
                if not stages(i)[0]:
                    return
                if past(i, 1):
                    pool.wait_ge(rot_ready, c(0))
                rot = ROT[:, bass.ds(i, 1), :].rearrange("p a b -> p (a b)")
                pool.tensor_tensor(TAB[:, :], rot, QKS[:, :], ALU.mult).then_inc(tab_ready, 1)
                pool.wait_ge(tab_ready, c(1))
                pool.wait_ge(qn_ready, c(1))
                if past(i, 1):
                    pool.wait_ge(t1_ready, c(0))
                half = DH // 2
                for k in range(2):
                    for h in range(2):
                        t = TAB[:, (2 * k + 1) * DH + h * half:(2 * k + 1) * DH + (h + 1) * half]
                        ins = pool.tensor_tensor(paired(V[:, k])[:, :, :, h * half:(h + 1) * half],
                                                 split(QN[:, k])[:, :, :, (1 - h) * half:(2 - h) * half],
                                                 per_dim(t, half), ALU.mult)
                ins.then_inc(vv_ready, 1)
                pool.wait_ge(u_ready, c(1))
                pool.wait_ge(vv_ready, c(1))
                for k in range(2):
                    ins = pool.tensor_tensor(V[:, k], V[:, k], U[:, k], ALU.add)
                ins.then_inc(rot_ready, 1)

            def ffn(inv, lay, start_next):
                pass

            stack = layers(pool, step, attn_start, ffn)
            stack(0)
            stack(1)

        @block.sync
        def _(sp):
            for t, n in ((EYE, "c_eye"), (CENTER, "c_center"), (BLOCKS, "c_blocks"), (NEXT, "c_next")):
                sp.dma_start(t[:, :], a[n]).then_inc(consts, 16)
            sp.dma_start(MASKF[:, :, :].rearrange("p a b -> p (a b)"), a["c_masks"]).then_inc(consts, 16)
            sp.dma_start(XIO, a["x"].rearrange("b (c p) d -> p (b c) d", p=P)).then_inc(x_in, 16)
            sp.dma_start(ROT[:, :, :].rearrange("p a b -> p (a b)"), a["c_rot"]).then_inc(consts, 16)

            def load_attn(lay):
                sp.dma_start(WQKV[:, :], a["wqkv"][bass.ds(lay, 1)].rearrange("l p n -> p (l n)")).then_inc(attn_w, 16)
                sp.dma_start(WO[:, :, :], a["wo"][bass.ds(lay, 1)].rearrange("l (h p) n -> p (l h) n", p=P)).then_inc(attn_w, 16)
                sp.dma_start(QKS[:, :], a["qks"][bass.ds(lay, 1), :].broadcast_to([P, 4 * DH])).then_inc(attn_w, 16)

            def load_ffn(lay):
                sp.dma_start(W1[:, :], a["w1"][bass.ds(lay, 1)].rearrange("l p n -> p (l n)")).then_inc(ffn_w, 16)
                sp.dma_start(W2[0:FT[0][1], 0:2, :],
                             a["w2"][bass.ds(lay, 1), 0:FT[2][0]].rearrange("l (i p) n -> p (l i) n", i=2)).then_inc(ffn_w, 16)
                sp.dma_start(W2[0:FT[2][1], 2, :],
                             a["w2"][bass.ds(lay, 1), FT[2][0]:DI].rearrange("l p n -> p (l n)")).then_inc(ffn_w, 16)
                sp.dma_start(SMALL[:, :], a["small"][bass.ds(lay, 1)].rearrange("l p n -> p (l n)")).then_inc(ffn_w, 16)

            load_attn(0)
            for t, n in ((WQM, "m_q"), (WKVM, "m_kv"), (PROJ, "m_proj"), (FC1, "m_fc1"), (MSMALL, "m_small")):
                sp.dma_start(t[:, :], a[n]).then_inc(mid_w, 16)
            sp.dma_start(FC2[:, :, :], a["m_fc2"].rearrange("(n p) d -> p n d", p=P)).then_inc(mid_w, 16)

            def attn_start(inv, lay):
                sp.wait_ge(init, 5)
                if inv == 0:
                    sp.wait_ge(xa_ready, sp.snap(lay * 4 + 4))
                else:
                    sp.wait_ge(xa_ready, sp.snap(lay * 4 + (DEPTH * 4 + 8)))
                load_ffn(lay)

            def step(p, i, c, v2, within=None, part=None):
                if not stages(i)[0]:
                    return
                done = v2_odd if p else v2_even
                sp.wait_ge(v_evac, c(1))
                sp.wait_ge(o_ready, c(1))
                for r in range(2):
                    cols = slice(r * 512, (r + 1) * 512)
                    for w in range(NW):
                        own = VS[WIN * w:WIN * (w + 1), p, cols]
                        before = VS[WIN * (w - 1):WIN * w, p, cols] if w else VS[P - WIN:P, 1 - p, cols]
                        sp.dma_start(V2[DH * r:DH * r + WIN, p, w, :], before).then_inc(done, 16)
                        sp.dma_start(V2[DH * r + WIN:DH * (r + 1), p, w, :], own).then_inc(done, 16)

            def ffn(inv, lay, start_next):
                sp.wait_ge(init, 5)
                sp.wait_ge(xb_ready, sp.snap(lay * CH + (inv * DEPTH + 1) * CH))
                load_attn(lay + 1)

            sp.wait_ge(init, 5)
            sp.wait_ge(halo_ready, 1)
            stack = layers(sp, step, attn_start, ffn)
            stack(0)
            stack(1)
            sp.wait_ge(attn_w, 16 * A_DMAS * (2 * DEPTH + 1))
            for b in range(4):
                sp.wait_ge(o_c, b + 1)
                sp.dma_start(out.rearrange("b (c p) d -> p (b c) d", p=P)[:, 4 * b:4 * b + 4, :],
                             XIO[:, 4 * b:4 * b + 4, :]).then_inc(stored, 16)
            sp.wait_ge(stored, 16 * 4)


def kernel(**inputs):
    import concourse.bacc as bacc
    from concourse.bass_utils import run_bass_kernel_spmd

    def get(name):
        return np.ascontiguousarray(inputs[name])

    def again(w):
        return np.concatenate([w, w[:1]], 0)

    def swapped(w):
        return np.concatenate([w[:, DH // 2:], w[:, :DH // 2]], 1)

    def tiles(v):
        cols = np.zeros((v.shape[0], P, 3), v.dtype)
        for n, (at, rows) in enumerate(FT):
            cols[:, :rows, n] = v[:, at:at + rows]
        return cols

    b1 = get("L0_ffn_b1")
    qs, ks = get("L0_ffn_q_scale"), get("L0_ffn_k_scale")
    small = np.concatenate([get("L0_ffn_ln_g")[:, :, None], get("L0_ffn_ln_b")[:, :, None],
                            get("L0_ffn_b2")[:, :, None], tiles(b1[:, :DI]), tiles(b1[:, DI:])], 2)
    mid = np.concatenate([get(n).reshape(P, 1) for n in (
        "L0_attn_norm1_g", "L0_attn_norm1_b", "L0_attn_proj_b", "L0_attn_norm2_g", "L0_attn_norm2_b",
        "L0_attn_fc2_b")] + [get("L0_attn_fc1_b").reshape(4, P).T], 1)
    arrays = {
        "x": get("L0_attn_x"),
        "wqkv": again(get("L0_ffn_Wqkv")), "wo": again(get("L0_ffn_Wo")),
        "qks": again(np.concatenate([qs, swapped(qs), ks, swapped(ks)], 1)),
        "w1": get("L0_ffn_W1"), "w2": get("L0_ffn_W2"), "small": small,
        "m_q": get("L0_attn_qkv_w")[:P].T, "m_kv": get("L0_attn_qkv_w")[P:].T,
        "m_proj": get("L0_attn_proj_w").T, "m_fc1": get("L0_attn_fc1_w").T, "m_fc2": get("L0_attn_fc2_w").T,
        "m_small": mid, **shape_constants(),
    }
    arrays = {n: np.ascontiguousarray(v) for n, v in arrays.items()}
    nc = bacc.Bacc("TRN2", target_bir_lowering=False, num_devices=1)
    aps = {n: nc.dram_tensor(n, v.shape, mybir.dt.from_np(v.dtype), kind="ExternalInput").ap() for n, v in arrays.items()}
    out = nc.dram_tensor("out", (1, NTOK, P), F32, kind="ExternalOutput").ap()
    build(nc, aps, out)
    got = run_bass_kernel_spmd(nc, [arrays], core_ids=[0])
    return got.results[0]["out"]
```
